# Optimizing a Trainium2 kernel written in Bass

```python
import numpy as np
import jax
import jax.numpy as jnp

def _softmax(x, axis=-1):
    return jax.nn.softmax(x, axis=axis)

def _gelu(x):
    return jax.nn.gelu(x, approximate=True)

def _silu(x):
    return jax.nn.silu(x)

def _sigmoid(x):
    return jax.nn.sigmoid(x)

def _layernorm(x, axis=-1, eps=1e-05):
    m = jnp.mean(x, axis=axis, keepdims=True)
    v = jnp.var(x, axis=axis, keepdims=True)
    return (x - m) / jnp.sqrt(v + eps)

def _scatter_add(tgt, idx, src, axis=0):
    return tgt.at[idx].add(src)

def _segment_sum(src, seg, n):
    return jax.ops.segment_sum(src, seg, n)
kernel_name = 'mk_seq_postln_d2_jaxref_r8_0b02cb'

def setup_inputs(seed: int=0):
    np.random.seed(seed)
    _w = jnp.asarray

    def _L0_attn_setup():
        import jax, jax.numpy as jnp
        import numpy as np
        D_MODEL = 128
        D_STATE = 16
        D_CONV = 4
        EXPAND = 1
        D_INNER = EXPAND * D_MODEL
        BATCH = 2
        SEQ = 256

        def silu(x):
            return x * jax.nn.sigmoid(x)
        key = jax.random.key(seed)
        ks = jax.random.split(key, 8)
        s = 0.02
        return {'x': jax.random.normal(ks[0], (BATCH, SEQ, D_MODEL), dtype=jnp.float32), 'W_in': jax.random.normal(ks[1], (2 * D_INNER, D_MODEL), dtype=jnp.float32) * s, 'conv_w': jax.random.normal(ks[2], (D_INNER, D_CONV), dtype=jnp.float32) * s, 'conv_b': jnp.zeros((D_INNER,), dtype=jnp.float32), 'W_dt': jax.random.normal(ks[3], (D_INNER, D_INNER), dtype=jnp.float32) * s, 'b_dt': jnp.zeros((D_INNER,), dtype=jnp.float32), 'A_log': jnp.zeros((D_INNER, D_STATE), dtype=jnp.float32), 'Bp': jax.random.normal(ks[4], (D_INNER, D_STATE), dtype=jnp.float32), 'Cp': jax.random.normal(ks[5], (D_INNER, D_STATE), dtype=jnp.float32), 'Dp': jnp.ones((D_INNER,), dtype=jnp.float32), 'W_out': jax.random.normal(ks[6], (D_MODEL, D_INNER), dtype=jnp.float32) * s}
    _L0_attn_in = _L0_attn_setup()

    def _L0_ffn_setup():
        import jax, jax.numpy as jnp
        import numpy as np
        D_IN, D_HID = (128, 512)

        def _ternary(key, shape):
            return jax.random.randint(key, shape, -1, 2).astype(jnp.float32)

        def _tlin(x, w, s):
            return jnp.einsum('bsi,oi->bso', x, w) * s
        key = jax.random.key(seed)
        ks = jax.random.split(key, 12)
        inv = lambda fan: 1.0 / np.sqrt(fan).astype(np.float32)
        return {'x': jax.random.normal(ks[0], (4, 256, D_IN), dtype=jnp.float32), 'w1_w': _ternary(ks[1], (D_HID, D_IN)), 'w1_s': jax.random.uniform(ks[2], (D_HID,), dtype=jnp.float32) * inv(D_IN), 'w2_w': _ternary(ks[3], (D_HID, D_IN)), 'w2_s': jax.random.uniform(ks[4], (D_HID,), dtype=jnp.float32) * inv(D_IN), 'h1_w': _ternary(ks[5], (D_HID, D_HID)), 'h1_s': jax.random.uniform(ks[6], (D_HID,), dtype=jnp.float32) * inv(D_HID), 'h2_w': _ternary(ks[7], (D_HID, D_HID)), 'h2_s': jax.random.uniform(ks[8], (D_HID,), dtype=jnp.float32) * inv(D_HID), 'w3_w': _ternary(ks[9], (D_IN, D_HID)), 'w3_s': jax.random.uniform(ks[10], (D_IN,), dtype=jnp.float32) * inv(D_HID)}
    _L0_ffn_in = _L0_ffn_setup()

    def _L1_attn_setup():
        import jax, jax.numpy as jnp
        import numpy as np
        B, N, DIM = (4, 128, 128)
        H, DH = (16, 64)
        NUM_MEM = 4
        TOPK = 64
        QK_SCALE = 10.0

        def l2norm(t, eps=1e-12):
            return t / jnp.clip(jnp.linalg.norm(t, axis=-1, keepdims=True), eps)
        key = jax.random.key(seed)
        ks = jax.random.split(key, 12)
        s = 0.02
        inp = {'x': jax.random.normal(ks[0], (B, N, DIM), dtype=jnp.float32), 'Wq': jax.random.normal(ks[1], (DIM, H * DH), dtype=jnp.float32) * s, 'Wk': jax.random.normal(ks[2], (DIM, H * DH), dtype=jnp.float32) * s, 'Wv': jax.random.normal(ks[3], (DIM, H * DH), dtype=jnp.float32) * s, 'W_pre_th': jax.random.normal(ks[4], (H, H), dtype=jnp.float32) * (1.0 / H) ** 0.5, 'W_post_th': jax.random.normal(ks[5], (H, H), dtype=jnp.float32) * (1.0 / H) ** 0.5, 'mem_k': jax.random.normal(ks[6], (H, NUM_MEM, DH), dtype=jnp.float32), 'mem_v': jax.random.normal(ks[7], (H, NUM_MEM, DH), dtype=jnp.float32), 'head_scale_params': jnp.ones((1, H, 1, 1), dtype=jnp.float32), 'Wg': jax.random.normal(ks[8], (DIM, H * DH), dtype=jnp.float32) * s, 'bg': jnp.ones((H * DH,), dtype=jnp.float32), 'Wo': jax.random.normal(ks[9], (H * DH, DIM), dtype=jnp.float32) * s}
        return inp
    _L1_attn_in = _L1_attn_setup()

    def _L1_ffn_setup():
        import jax, jax.numpy as jnp
        import numpy as np
        D_IN, D_HID = (128, 512)

        def _ternary(key, shape):
            return jax.random.randint(key, shape, -1, 2).astype(jnp.float32)

        def _tlin(x, w, s):
            return jnp.einsum('bsi,oi->bso', x, w) * s
        key = jax.random.key(seed)
        ks = jax.random.split(key, 12)
        inv = lambda fan: 1.0 / np.sqrt(fan).astype(np.float32)
        return {'x': jax.random.normal(ks[0], (4, 256, D_IN), dtype=jnp.float32), 'w1_w': _ternary(ks[1], (D_HID, D_IN)), 'w1_s': jax.random.uniform(ks[2], (D_HID,), dtype=jnp.float32) * inv(D_IN), 'w2_w': _ternary(ks[3], (D_HID, D_IN)), 'w2_s': jax.random.uniform(ks[4], (D_HID,), dtype=jnp.float32) * inv(D_IN), 'h1_w': _ternary(ks[5], (D_HID, D_HID)), 'h1_s': jax.random.uniform(ks[6], (D_HID,), dtype=jnp.float32) * inv(D_HID), 'h2_w': _ternary(ks[7], (D_HID, D_HID)), 'h2_s': jax.random.uniform(ks[8], (D_HID,), dtype=jnp.float32) * inv(D_HID), 'w3_w': _ternary(ks[9], (D_IN, D_HID)), 'w3_s': jax.random.uniform(ks[10], (D_IN,), dtype=jnp.float32) * inv(D_HID)}
    _L1_ffn_in = _L1_ffn_setup()
    _d = {'L0_attn_x': _L0_attn_in['x'], 'L0_attn_W_in': _L0_attn_in['W_in'], 'L0_attn_conv_w': _L0_attn_in['conv_w'], 'L0_attn_conv_b': _L0_attn_in['conv_b'], 'L0_attn_W_dt': _L0_attn_in['W_dt'], 'L0_attn_b_dt': _L0_attn_in['b_dt'], 'L0_attn_A_log': _L0_attn_in['A_log'], 'L0_attn_Bp': _L0_attn_in['Bp'], 'L0_attn_Cp': _L0_attn_in['Cp'], 'L0_attn_Dp': _L0_attn_in['Dp'], 'L0_attn_W_out': _L0_attn_in['W_out'], 'L0_ffn_w1_w': _L0_ffn_in['w1_w'], 'L0_ffn_w1_s': _L0_ffn_in['w1_s'], 'L0_ffn_w2_w': _L0_ffn_in['w2_w'], 'L0_ffn_w2_s': _L0_ffn_in['w2_s'], 'L0_ffn_h1_w': _L0_ffn_in['h1_w'], 'L0_ffn_h1_s': _L0_ffn_in['h1_s'], 'L0_ffn_h2_w': _L0_ffn_in['h2_w'], 'L0_ffn_h2_s': _L0_ffn_in['h2_s'], 'L0_ffn_w3_w': _L0_ffn_in['w3_w'], 'L0_ffn_w3_s': _L0_ffn_in['w3_s'], 'L1_attn_Wq': _L1_attn_in['Wq'], 'L1_attn_Wk': _L1_attn_in['Wk'], 'L1_attn_Wv': _L1_attn_in['Wv'], 'L1_attn_W_pre_th': _L1_attn_in['W_pre_th'], 'L1_attn_W_post_th': _L1_attn_in['W_post_th'], 'L1_attn_mem_k': _L1_attn_in['mem_k'], 'L1_attn_mem_v': _L1_attn_in['mem_v'], 'L1_attn_head_scale_params': _L1_attn_in['head_scale_params'], 'L1_attn_Wg': _L1_attn_in['Wg'], 'L1_attn_bg': _L1_attn_in['bg'], 'L1_attn_Wo': _L1_attn_in['Wo'], 'L1_ffn_w1_w': _L1_ffn_in['w1_w'], 'L1_ffn_w1_s': _L1_ffn_in['w1_s'], 'L1_ffn_w2_w': _L1_ffn_in['w2_w'], 'L1_ffn_w2_s': _L1_ffn_in['w2_s'], 'L1_ffn_h1_w': _L1_ffn_in['h1_w'], 'L1_ffn_h1_s': _L1_ffn_in['h1_s'], 'L1_ffn_h2_w': _L1_ffn_in['h2_w'], 'L1_ffn_h2_s': _L1_ffn_in['h2_s'], 'L1_ffn_w3_w': _L1_ffn_in['w3_w'], 'L1_ffn_w3_s': _L1_ffn_in['w3_s']}
    _x0 = _d['L0_attn_x']
    _d['L0_attn_x'] = jax.random.normal(jax.random.fold_in(jax.random.key(seed), 1), (32, 256, 128), dtype=_x0.dtype)
    del _x0
    return _d

def reference(L0_attn_x, L0_attn_W_in, L0_attn_conv_w, L0_attn_conv_b, L0_attn_W_dt, L0_attn_b_dt, L0_attn_A_log, L0_attn_Bp, L0_attn_Cp, L0_attn_Dp, L0_attn_W_out, L0_ffn_w1_w, L0_ffn_w1_s, L0_ffn_w2_w, L0_ffn_w2_s, L0_ffn_h1_w, L0_ffn_h1_s, L0_ffn_h2_w, L0_ffn_h2_s, L0_ffn_w3_w, L0_ffn_w3_s, L1_attn_Wq, L1_attn_Wk, L1_attn_Wv, L1_attn_W_pre_th, L1_attn_W_post_th, L1_attn_mem_k, L1_attn_mem_v, L1_attn_head_scale_params, L1_attn_Wg, L1_attn_bg, L1_attn_Wo, L1_ffn_w1_w, L1_ffn_w1_s, L1_ffn_w2_w, L1_ffn_w2_s, L1_ffn_h1_w, L1_ffn_h1_s, L1_ffn_h2_w, L1_ffn_h2_s, L1_ffn_w3_w, L1_ffn_w3_s):

    def _L0_attn_ref(x, W_in, conv_w, conv_b, W_dt, b_dt, A_log, Bp, Cp, Dp, W_out):
        import jax, jax.numpy as jnp
        import numpy as np
        D_MODEL = 128
        D_STATE = 16
        D_CONV = 4
        EXPAND = 1
        D_INNER = EXPAND * D_MODEL
        BATCH = 2
        SEQ = 256

        def silu(x):
            return x * jax.nn.sigmoid(x)
        B, L, _ = x.shape
        xr = x @ W_in.T
        x_proj, res = jnp.split(xr, 2, axis=-1)
        xp = jnp.pad(x_proj, ((0, 0), (D_CONV - 1, 0), (0, 0)))
        xc = conv_b + sum((conv_w[:, k] * xp[:, k:k + L, :] for k in range(D_CONV)))
        xc = silu(xc)
        delta = jax.nn.softplus(xc @ W_dt.T + b_dt)
        A = -jnp.exp(A_log)
        dA = jnp.exp(delta[..., None] * A)
        dBx = delta[..., None] * Bp * xc[..., None]

        def step(h, inp):
            dA_t, dBx_t = inp
            h = dA_t * h + dBx_t
            y = jnp.einsum('bdn,dn->bd', h, Cp)
            return (h, y)
        h0 = jnp.zeros((B, D_INNER, D_STATE), dtype=x.dtype)
        _, ys = jax.lax.scan(step, h0, (dA.transpose(1, 0, 2, 3), dBx.transpose(1, 0, 2, 3)))
        x_ssm = ys.transpose(1, 0, 2) + xc * Dp
        return x_ssm * silu(res) @ W_out.T

    def _L0_ffn_ref(x, w1_w, w1_s, w2_w, w2_s, h1_w, h1_s, h2_w, h2_s, w3_w, w3_s):
        import jax, jax.numpy as jnp
        import numpy as np
        D_IN, D_HID = (128, 512)

        def _ternary(key, shape):
            return jax.random.randint(key, shape, -1, 2).astype(jnp.float32)

        def _tlin(x, w, s):
            return jnp.einsum('bsi,oi->bso', x, w) * s
        h = jax.nn.silu(_tlin(x, w1_w, w1_s)) * _tlin(x, w2_w, w2_s)
        h = jax.nn.gelu(_tlin(h, h1_w, h1_s), approximate=False)
        h = jax.nn.gelu(_tlin(h, h2_w, h2_s), approximate=False)
        return _tlin(h, w3_w, w3_s)

    def _L1_attn_ref(x, Wq, Wk, Wv, W_pre_th, W_post_th, mem_k, mem_v, head_scale_params, Wg, bg, Wo):
        import jax, jax.numpy as jnp
        import numpy as np
        B, N, DIM = (4, 128, 128)
        H, DH = (16, 64)
        NUM_MEM = 4
        TOPK = 64
        QK_SCALE = 10.0

        def l2norm(t, eps=1e-12):
            return t / jnp.clip(jnp.linalg.norm(t, axis=-1, keepdims=True), eps)
        b, n, _ = x.shape
        q = (x @ Wq).reshape(b, n, H, DH).transpose(0, 2, 1, 3)
        k = (x @ Wk).reshape(b, n, H, DH).transpose(0, 2, 1, 3)
        v = (x @ Wv).reshape(b, n, H, DH).transpose(0, 2, 1, 3)
        mk = jnp.broadcast_to(mem_k[None], (b, H, NUM_MEM, DH))
        mv = jnp.broadcast_to(mem_v[None], (b, H, NUM_MEM, DH))
        k = jnp.concatenate([mk, k], axis=2)
        v = jnp.concatenate([mv, v], axis=2)
        q = l2norm(q)
        k = l2norm(k)
        dots = jnp.einsum('bhid,bhjd->bhij', q, k) * QK_SCALE
        dots = jnp.einsum('hg,bgij->bhij', W_pre_th, dots)
        mask_value = -jnp.finfo(dots.dtype).max
        j = n + NUM_MEM
        col_pos = jnp.arange(j) - NUM_MEM
        causal = jnp.arange(n)[:, None] < col_pos[None, :]
        dots = jnp.where(causal[None, None], mask_value, dots)
        top = jax.lax.top_k(dots, TOPK)[0]
        vk = top[..., -1:]
        dots = jnp.where(dots < vk, mask_value, dots)
        attn = jax.nn.softmax(dots, axis=-1)
        attn = jnp.einsum('hg,bgij->bhij', W_post_th, attn)
        out = jnp.einsum('bhij,bhjd->bhid', attn, v)
        out = out * head_scale_params
        out = out.transpose(0, 2, 1, 3).reshape(b, n, H * DH)
        gates = x @ Wg + bg
        out = out * jax.nn.sigmoid(gates)
        return out @ Wo

    def _L1_ffn_ref(x, w1_w, w1_s, w2_w, w2_s, h1_w, h1_s, h2_w, h2_s, w3_w, w3_s):
        import jax, jax.numpy as jnp
        import numpy as np
        D_IN, D_HID = (128, 512)

        def _ternary(key, shape):
            return jax.random.randint(key, shape, -1, 2).astype(jnp.float32)

        def _tlin(x, w, s):
            return jnp.einsum('bsi,oi->bso', x, w) * s
        h = jax.nn.silu(_tlin(x, w1_w, w1_s)) * _tlin(x, w2_w, w2_s)
        h = jax.nn.gelu(_tlin(h, h1_w, h1_s), approximate=False)
        h = jax.nn.gelu(_tlin(h, h2_w, h2_s), approximate=False)
        return _tlin(h, w3_w, w3_s)
    x = L0_attn_x
    x = _layernorm(x + _L0_attn_ref(x, L0_attn_W_in, L0_attn_conv_w, L0_attn_conv_b, L0_attn_W_dt, L0_attn_b_dt, L0_attn_A_log, L0_attn_Bp, L0_attn_Cp, L0_attn_Dp, L0_attn_W_out), axis=-1)
    x = _layernorm(x + _L0_ffn_ref(x, L0_ffn_w1_w, L0_ffn_w1_s, L0_ffn_w2_w, L0_ffn_w2_s, L0_ffn_h1_w, L0_ffn_h1_s, L0_ffn_h2_w, L0_ffn_h2_s, L0_ffn_w3_w, L0_ffn_w3_s), axis=-1)
    x = _layernorm(x + _L1_attn_ref(x, L1_attn_Wq, L1_attn_Wk, L1_attn_Wv, L1_attn_W_pre_th, L1_attn_W_post_th, L1_attn_mem_k, L1_attn_mem_v, L1_attn_head_scale_params, L1_attn_Wg, L1_attn_bg, L1_attn_Wo), axis=-1)
    x = _layernorm(x + _L1_ffn_ref(x, L1_ffn_w1_w, L1_ffn_w1_s, L1_ffn_w2_w, L1_ffn_w2_s, L1_ffn_h1_w, L1_ffn_h1_s, L1_ffn_h2_w, L1_ffn_h2_s, L1_ffn_w3_w, L1_ffn_w3_s), axis=-1)
    return x

_drawn_inputs = setup_inputs


def setup_inputs(seed=0):
    import zlib

    import numpy as np

    out = dict(_drawn_inputs(seed))
    spreads = {'L0_attn_conv_b': (0.0, 0.8),
     'L0_attn_b_dt': (0.0, 0.8),
     'L0_attn_A_log': (0.0, 0.8),
     'L0_attn_Dp': (1.0, 0.6),
     'L1_attn_head_scale_params': (1.0, 0.6),
     'L1_attn_bg': (1.0, 0.6)}
    factors = {'L0_attn_W_in': 7.159,
     'L0_attn_conv_w': 8.0,
     'L0_attn_W_dt': 8.0,
     'L0_attn_Bp': 6.939,
     'L0_attn_Cp': 6.66,
     'L0_attn_W_out': 7.157,
     'L0_ffn_w1_w': 8.0,
     'L0_ffn_w1_s': 8.0,
     'L0_ffn_w2_w': 8.0,
     'L0_ffn_w2_s': 8.0,
     'L0_ffn_h1_w': 8.0,
     'L0_ffn_h1_s': 8.0,
     'L0_ffn_h2_w': 8.0,
     'L0_ffn_h2_s': 8.0,
     'L0_ffn_w3_w': 8.0,
     'L0_ffn_w3_s': 8.0,
     'L1_attn_Wg': 8.0,
     'L1_ffn_w1_w': 8.0,
     'L1_ffn_w1_s': 8.0,
     'L1_ffn_w2_w': 8.0,
     'L1_ffn_w2_s': 8.0,
     'L1_ffn_h1_w': 8.0,
     'L1_ffn_h1_s': 8.0,
     'L1_ffn_h2_w': 8.0,
     'L1_ffn_h2_s': 8.0,
     'L1_ffn_w3_w': 8.0,
     'L1_ffn_w3_s': 8.0}
    for name, (base, spread) in spreads.items():
        noise = np.random.default_rng([zlib.crc32(name.encode()), seed]).standard_normal(out[name].shape)
        drawn = base * np.exp(spread * noise) if base else spread * noise
        out[name] = jnp.asarray(drawn.astype(out[name].dtype))
    for name, factor in factors.items():
        out[name] = (out[name] * factor).astype(out[name].dtype)
    return out
```

```python
from contextlib import ExitStack

import numpy as np

import concourse.bass as bass
from concourse import mybir

F32 = mybir.dt.float32
ALU = mybir.AluOpType
ACT = mybir.ActivationFunctionType

P = 128
SEQS, SEQ = 32, 256
STATES, TAPS = 16, 4
HID = 512
HC = HID // P
HEADS, DH, MEM, TOPK = 16, 64, 4, 64
INNER = HEADS * DH
IC = INNER // P
KEYS = MEM + SEQ
QG = P // HEADS
GROUPS = SEQ // QG
QK_SCALE = 10.0
LN_EPS = 1e-5
NORM_EPS = 1e-12
MASKED = float(np.finfo(np.float32).min)
HALF = GROUPS // 2
W_LO, W_HI = MEM + P, KEYS


def seen_by(group):
    return MEM + QG * (group + 1)


class Engine:

    def __init__(self, engine, sem):
        self.engine, self.sem, self.count, self.waited = engine, sem, 0, {}

    def wait(self, *marks):
        for sem, value in marks:
            if self.waited.get(sem.name, 0) < value:
                self.waited[sem.name] = value
                self.engine.wait_ge(sem, value)

    def do(self, step):
        self.count += 1
        step(self.engine).then_inc(self.sem, 1)
        return (self.sem, self.count)

    def quiet(self, step):
        step(self.engine)


class Dma:

    def __init__(self, sem):
        self.sem, self.count = sem, 0

    def start(self, queue, out, in_):
        self.count += 16
        queue.engine.dma_start(out, in_).then_inc(self.sem, 16)
        return (self.sem, self.count)


class Banks:

    def __init__(self, banks):
        self.banks, self.at, self.freed = banks, 0, [None] * len(banks)

    def take(self, engine):
        n = self.at % len(self.banks)
        self.at += 1
        if self.freed[n] == "open":
            raise AssertionError("a PSUM bank is taken before its reader is queued")
        if self.freed[n] is not None:
            engine.wait(self.freed[n])
        self.freed[n] = "open"
        return self.banks[n], n

    def free(self, n, mark):
        self.freed[n] = mark


BLOCKED = "blocked"
DONE = "done"


def interleave(actors):
    live = [{"gen": gen, "per": per, "lag": lag, "whole": 0, "part": 0.0} for gen, per, lag in actors]
    stuck = []
    while live:
        ready = [a for a in live if a not in stuck]
        if not ready:
            raise AssertionError("every actor is blocked")
        a = min(ready, key=lambda a: a["whole"] + min(a["part"], 1.0) + a["lag"])
        said = next(a["gen"], "ended")
        if said == BLOCKED:
            stuck.append(a)
            continue
        stuck = []
        if said == "ended":
            live.remove(a)
        elif said == DONE:
            a["whole"], a["part"] = a["whole"] + 1, 0.0
        else:
            a["part"] += (1 if said is None else said) / a["per"]


def program(nc, d, out):
    with ExitStack() as ctx:
        n_sem = [0]

        def sem(name):
            n_sem[0] += 1
            return ctx.enter_context(nc.semaphore(name))

        def sb(name, shape, dt=F32, scope=ctx):
            return scope.enter_context(nc.sbuf_tensor(name, shape, dt))

        pe, act = Engine(nc.tensor, sem("pe_done")), Engine(nc.scalar, sem("act_done"))
        dve, pool = Engine(nc.vector, sem("dve_done")), Engine(nc.gpsimd, sem("pool_done"))
        sp = Engine(nc.sync, sem("sp_done"))
        bank = [ctx.enter_context(nc.psum_tensor(f"bank{i}", [P, 512], F32)) for i in range(8)]
        x_mid = nc.dram_tensor("x_mid", [P, SEQS * SEQ], F32).ap()

        def matmul(o, l, r, start=True, stop=True):
            return lambda e: e.matmul(o, l, r, start=start, stop=stop)

        weights = {0: Dma(sem("weights0_in")), 1: Dma(sem("weights1_in"))}

        def load(name, shape, scope=ctx, block=0):
            t = sb("w_" + name, shape, scope=scope)
            return t, weights[block].start(sp, t[:], d[name])

        ident, _ = load("ident", [P, P])
        meanmat, consts_in = load("meanmat", [P, P])
        eps = sb("eps", [P, 1])
        eps_set = pool.do(lambda e: e.memset(eps[:], LN_EPS))

        ln_cen = [sb(f"ln_cen{i}", [P, SEQ]) for i in range(2)]
        ln_sq = [sb(f"ln_sq{i}", [P, SEQ]) for i in range(2)]
        ln_sd = [sb(f"ln_sd{i}", [P, 2]) for i in range(2)]
        ln_rs = [sb(f"ln_rs{i}", [P, 2]) for i in range(2)]

        def layer_norm(r, r_ready, slot, banks, result, result_free=()):
            cen, sq, sd, rs = ln_cen[slot], ln_sq[slot], ln_sd[slot], ln_rs[slot]
            pe.wait(r_ready)
            mean, n = banks.take(pe)
            meaned = pe.do(matmul(mean[:, 0:SEQ], meanmat[:], r))
            yield
            dve.wait(meaned)
            centred = dve.do(lambda e: e.tensor_tensor(cen[:], r, mean[:, 0:SEQ], ALU.subtract))
            banks.free(n, centred)
            act.wait(centred)
            squared = act.do(lambda e: e.activation(sq[:], cen[:], ACT.Square))
            yield
            pe.wait(squared)
            var, n = banks.take(pe)
            for t in range(2):
                step = matmul(var[:, t:t + 1], sq[:, t * P:(t + 1) * P], meanmat[:, 0:1])
                varied = pe.do(step)
            yield
            act.wait(varied, eps_set)
            rooted = act.do(lambda e: e.activation(sd[:], var[:, 0:2], ACT.Sqrt, bias=eps[:, 0:1]))
            banks.free(n, rooted)
            dve.wait(rooted)
            inverted = dve.do(lambda e: e.reciprocal(rs[:], sd[:]))
            yield
            pe.wait(inverted)
            spread, n = banks.take(pe)
            for t in range(2):
                step = matmul(spread[:, t * P:(t + 1) * P], rs[:, t:t + 1].to_broadcast([P, P]), ident[:])
                spreaded = pe.do(step)
            yield
            dve.wait(spreaded, *result_free)
            normed = dve.do(lambda e: e.tensor_tensor(result, cen[:], spread[:, 0:SEQ], ALU.mult))
            banks.free(n, normed)
            return normed

        def load_ffn(b, scope):
            w, block = {}, int(b[1])
            w["w1"], _ = load(f"{b}w1", [P, HID], scope, block)
            w["w2"], _ = load(f"{b}w2", [P, HID], scope, block)
            for k in ("h1", "h2"):
                w[k], _ = load(b + k, [P, HC, HID], scope, block)
            w["w3"], _ = load(f"{b}w3", [P, HC, P], scope, block)
            w["s"], w["in"] = load(f"{b}s", [P, 4 * HC + 1], scope, block)
            return w

        def ffn(w, h, x, x_ready, banks, r_free, r):
            scale = lambda k, m: w["s"][:, k * HC + m:k * HC + m + 1]
            pe.wait(x_ready, w["in"])
            gated = []
            for m2 in range(HC // 2):
                pair = []
                for k in ("w1", "w2"):
                    o, n = banks.take(pe)
                    for m in range(2):
                        c = (2 * m2 + m) * P
                        made = pe.do(matmul(o[:, m * SEQ:(m + 1) * SEQ], w[k][:, c:c + P], x))
                    pair.append((o, n, made))
                yield
                (a, an, a_made), (b, bn, b_made) = pair
                act.wait(a_made, *h["free"])
                for m in range(2):
                    silued = act.do(lambda e, m=m: e.activation(h["act"][:, m, :], a[:, m * SEQ:(m + 1) * SEQ],
                                                                ACT.Silu, scale=scale(0, 2 * m2 + m)))
                banks.free(an, silued)
                yield
                dve.wait(silued, b_made)
                for m in range(2):
                    g = dve.do(lambda e, m=m: e.scalar_tensor_tensor(
                        out=h["a"][:, 2 * m2 + m, :], in0=b[:, m * SEQ:(m + 1) * SEQ], scalar=scale(1, 2 * m2 + m),
                        in1=h["act"][:, m, :], op0=ALU.mult, op1=ALU.mult))
                banks.free(bn, g)
                h["free"] = (g,)
                gated.append(g)
                yield
            src, ready = h["a"], gated[-1]
            for k, layer, dst in ((2, "h1", h["b"]), (3, "h2", h["a"])):
                pe.wait(ready)
                for m2 in range(HC // 2):
                    o, n = banks.take(pe)
                    for m in range(2):
                        for c in range(HC):
                            step = matmul(o[:, m * SEQ:(m + 1) * SEQ], w[layer][:, c, (2 * m2 + m) * P:(2 * m2 + m + 1) * P],
                                          src[:, c, :], start=c == 0, stop=c == HC - 1)
                            if c < HC - 1:
                                pe.quiet(step)
                            else:
                                made = pe.do(step)
                        yield
                    act.wait(made)
                    for m in range(2):
                        ready = act.do(lambda e, m=m: e.activation(dst[:, 2 * m2 + m, :], o[:, m * SEQ:(m + 1) * SEQ],
                                                                   ACT.Gelu, scale=scale(k, 2 * m2 + m)))
                    banks.free(n, ready)
                    yield
                src = dst
            pe.wait(ready)
            o, n = banks.take(pe)
            for c in range(HC):
                step = matmul(o[:, 0:SEQ], w["w3"][:, c, :], src[:, c, :], start=c == 0, stop=c == HC - 1)
                if c < HC - 1:
                    pe.quiet(step)
                else:
                    made = pe.do(step)
            yield
            dve.wait(made, *r_free)
            added = dve.do(lambda e: e.scalar_tensor_tensor(out=r, in0=o[:, 0:SEQ], scalar=w["s"][:, 4 * HC:4 * HC + 1],
                                                            in1=x, op0=ALU.mult, op1=ALU.add))
            banks.free(n, added)
            return added

        with ExitStack() as blk:
            sb0 = lambda name, shape: sb(name, shape, scope=blk)
            w_in, _ = load("w_in", [P, P], scope=blk)
            w_res, _ = load("w_resT", [P, P], scope=blk)
            w_dt, _ = load("w_dtT", [P, P], scope=blk)
            w_out, _ = load("w_outT", [P, P], scope=blk)
            vec, _ = load("vec", [P, 7], scope=blk)
            ssm, _ = load("ssm", [P, 3 * STATES], scope=blk)
            w0 = load_ffn("f0", blk)
            w0_in = w0["in"]
            conv_b, b_dt, Dp = vec[:, 4:5], vec[:, 5:6], vec[:, 6:7]

            conv_d = sb0("conv_d", [P, TAPS, P])
            w_conv = sb0("w_conv", [P, TAPS, P])
            neg_a = sb0("neg_a", [P, STATES])
            bc = sb0("bc", [P, STATES])
            mix_d = sb0("mix_d", [P, STATES + 1, P])
            dve.wait(w0_in)
            for k in range(TAPS):
                tapped = dve.do(lambda e, k=k: e.tensor_scalar(conv_d[:, k, :], ident[:], vec[:, k:k + 1], None, ALU.mult))
            pe.wait(tapped)
            for k in range(TAPS):
                step = matmul(bank[0][:, k * P:(k + 1) * P], w_in[:], conv_d[:, k, :])
                folded = pe.do(step)
            dve.wait(folded)
            conv_ready = dve.do(lambda e: e.tensor_copy(w_conv[:].rearrange("p k n -> p (k n)"), bank[0][:]))
            act.wait(w0_in)
            a_made = act.do(lambda e: e.activation(neg_a[:], ssm[:, 0:STATES], ACT.Exp))
            dve.wait(a_made)
            a_ready = dve.do(lambda e: e.tensor_scalar(neg_a[:], neg_a[:], -1.0, None, ALU.mult))
            bc_made = dve.do(lambda e: e.tensor_tensor(bc[:], ssm[:, STATES:2 * STATES], ssm[:, 2 * STATES:3 * STATES], ALU.mult))
            dve.wait(bc_made)
            for s in range(STATES):
                dve.do(lambda e, s=s: e.tensor_scalar(mix_d[:, s, :], ident[:], bc[:, s:s + 1], None, ALU.mult))
            mix_ready = dve.do(lambda e: e.tensor_scalar(mix_d[:, STATES, :], ident[:], Dp, None, ALU.mult))

            NX = 3
            x_in = [sb0(f"x_in{i}", [P, 4 + SEQ]) for i in range(NX)]
            x_slot = [Dma(sem(f"x_in{i}")) for i in range(NX)]
            xc = [sb0(f"xc{i}", [P, SEQ]) for i in range(NX)]
            sres = [sb0(f"sres{i}", [P, SEQ]) for i in range(NX)]
            delta = [sb0(f"delta{i}", [P, SEQ]) for i in range(NX)]
            dx = [sb0(f"dx{i}", [P, SEQ]) for i in range(NX)]
            sp_t = [sb0(f"sp_t{i}", [P, SEQ]) for i in range(5)]
            ND = 4
            dA = [sb0(f"dA{i}", [P, SEQ]) for i in range(ND)]
            hs = [sb0(f"hs{i}", [P, SEQ]) for i in range(ND)]
            z = sb0("z", [P, SEQ])
            r0 = sb0("r0", [P, SEQ])
            x_a = [sb0(f"x_a{i}", [P, SEQ]) for i in range(2)]
            r1 = sb0("r1", [P, SEQ])
            x_b = [sb0(f"x_b{i}", [P, SEQ]) for i in range(2)]
            out_slot = [Dma(sem(f"mid_out{i}")) for i in range(2)]
            h0 = {"act": sb0("h_act", [P, 2, SEQ]), "a": sb0("h_a", [P, HC, SEQ]), "b": sb0("h_b", [P, HC, SEQ]), "free": ()}

            pads = [pool.do(lambda e, t=t: e.memset(t[:, 0:4], 0.0)) for t in x_in]
            front_banks, scan_banks, ffn_banks = Banks(bank[0:2]), Banks(bank[2:5]), Banks(bank[5:8])
            front_banks.free(0, conv_ready)
            m = {}

            def mixer_front():
                for b in range(SEQS):
                    i = b % NX
                    xt = x_in[i]
                    if b >= NX:
                        while ("x_used", b - NX) not in m:
                            yield BLOCKED
                        sp.wait(m["x_used", b - NX])
                    loaded = x_slot[i].start(sp, xt[:, 4:], d["xT"][:, b * SEQ:(b + 1) * SEQ])
                    pe.wait(loaded, conv_ready, pads[i], w0_in)
                    conv, cn = front_banks.take(pe)
                    for k in range(TAPS):
                        step = matmul(conv[:, 0:SEQ], w_conv[:, k, :], xt[:, 1 + k:1 + k + SEQ], start=k == 0, stop=k == TAPS - 1)
                        if k < TAPS - 1:
                            pe.quiet(step)
                        else:
                            conved = pe.do(step)
                    resed = pe.do(matmul(conv[:, SEQ:2 * SEQ], w_res[:], xt[:, 4:]))
                    yield
                    act.wait(resed)
                    if b >= NX:
                        while ("y_gated", b - NX) not in m:
                            yield BLOCKED
                        act.wait(m["y_gated", b - NX])
                    xc_made = act.do(lambda e: e.activation(xc[i][:], conv[:, 0:SEQ], ACT.Silu, bias=conv_b))
                    m["sres", b] = act.do(lambda e: e.activation(sres[i][:], conv[:, SEQ:2 * SEQ], ACT.Silu))
                    front_banks.free(cn, m["sres", b])
                    yield
                    pe.wait(xc_made)
                    dt, dn = front_banks.take(pe)
                    dted = pe.do(matmul(dt[:, 0:SEQ], w_dt[:], xc[i][:]))
                    yield
                    va, e_, u, lu, rl = sp_t
                    act.wait(dted)
                    if b:
                        act.wait(m["delta", b - 1])
                    absed = act.do(lambda e: e.activation(va[:], dt[:, 0:SEQ], ACT.Abs, bias=b_dt))
                    act.wait(absed)
                    exped = act.do(lambda e: e.activation(e_[:], va[:], ACT.Exp, scale=-1.0))
                    dve.wait(absed)
                    relued = dve.do(lambda e: e.tensor_scalar(rl[:], dt[:, 0:SEQ], b_dt, 0.0, ALU.add, ALU.max))
                    yield
                    dve.wait(exped)
                    front_banks.free(dn, relued)
                    u_made = dve.do(lambda e: e.tensor_scalar(u[:], e_[:], 1.0, None, ALU.add))
                    act.wait(u_made)
                    logged = act.do(lambda e: e.activation(lu[:], u[:], ACT.Ln))
                    dve.wait(u_made)
                    erred = dve.do(lambda e: e.scalar_tensor_tensor(out=va[:], in0=u[:], scalar=1.0, in1=e_[:],
                                                                    op0=ALU.subtract, op1=ALU.subtract))
                    dve.wait(erred, relued)
                    part = dve.do(lambda e: e.tensor_tensor(rl[:], rl[:], va[:], ALU.subtract))
                    yield
                    dve.wait(part, logged)
                    m["delta", b] = dve.do(lambda e: e.tensor_tensor(delta[i][:], rl[:], lu[:], ALU.add))
                    dve.wait(m["delta", b], xc_made)
                    m["dx", b] = dve.do(lambda e: e.tensor_tensor(dx[i][:], delta[i][:], xc[i][:], ALU.mult))
                    m["xc", b] = xc_made
                    yield DONE

            scanned_by = [None] * ND
            summed_by = [None] * ND

            def scan():
                k = 0
                for b in range(SEQS):
                    i = b % NX
                    while ("dx", b) not in m:
                        yield BLOCKED
                    y, yn = scan_banks.take(pe)
                    pe.wait(m["xc", b], mix_ready)
                    pe.quiet(matmul(y[:, 0:SEQ], mix_d[:, STATES, :], xc[i][:], start=True, stop=False))
                    scans = []
                    for s in range(STATES + 1):
                        if s < STATES:
                            j = k % ND
                            act.wait(m["delta", b], a_ready, *([scanned_by[j]] if scanned_by[j] else []))
                            decayed = act.do(lambda e, s=s, j=j: e.activation(dA[j][:], delta[i][:], ACT.Exp, scale=neg_a[:, s:s + 1]))
                            dve.wait(decayed, m["dx", b], *([summed_by[j]] if summed_by[j] else []))
                            scanned = dve.do(lambda e, j=j: e.tensor_tensor_scan(hs[j][:], dA[j][:], dx[i][:], 0.0, ALU.mult, ALU.add))
                            scanned_by[j] = scanned
                            scans.append((j, scanned))
                            k += 1
                        if s >= 1:
                            j, scanned = scans[s - 1]
                            pe.wait(scanned)
                            summed = pe.do(matmul(y[:, 0:SEQ], mix_d[:, s - 1, :], hs[j][:], start=False, stop=s == STATES))
                            summed_by[j] = summed
                        if s % 2:
                            yield
                    dve.wait(summed, m["sres", b])
                    gated = dve.do(lambda e: e.tensor_tensor(z[:], y[:, 0:SEQ], sres[i][:], ALU.mult))
                    m["y_gated", b] = gated
                    scan_banks.free(yn, gated)
                    yield
                    pe.wait(gated)
                    o, n = scan_banks.take(pe)
                    projected = pe.do(matmul(o[:, 0:SEQ], w_out[:], z[:]))
                    yield
                    dve.wait(projected)
                    added = dve.do(lambda e: e.tensor_tensor(r0[:], o[:, 0:SEQ], x_in[i][:, 4:], ALU.add))
                    scan_banks.free(n, added)
                    m["x_used", b] = added
                    free = ()
                    if b >= 2:
                        while ("x_a_used", b - 2) not in m:
                            yield BLOCKED
                        free = (m["x_a_used", b - 2],)
                    m["x_a", b] = yield from layer_norm(r0[:], added, 0, scan_banks, x_a[b % 2][:], free)
                    yield DONE

            def ffn0():
                for b in range(SEQS):
                    while ("x_a", b) not in m:
                        yield BLOCKED
                    added = yield from ffn(w0, h0, x_a[b % 2][:], m["x_a", b], ffn_banks, (), r1[:])
                    m["x_a_used", b] = added
                    free = (m["mid", b - 2],) if b >= 2 else ()
                    normed = yield from layer_norm(r1[:], added, 1, ffn_banks, x_b[b % 2][:], free)
                    sp.wait(normed)
                    m["mid", b] = out_slot[b % 2].start(sp, x_mid[:, b * SEQ:(b + 1) * SEQ], x_b[b % 2][:])
                    yield DONE

            interleave([(mixer_front(), 6, -1), (scan(), 16, 0), (ffn0(), 25, 1)])
            block0_stored = [m["mid", SEQS - 2], m["mid", SEQS - 1]]
            block0_ended = [(x.sem, x.count) for x in (pe, act, dve, pool)]

        for engine in (sp, pe, act, dve, pool):
            engine.wait(*block0_ended, *block0_stored)
        with ExitStack() as blk:
            sb1 = lambda name, shape: sb(name, shape, scope=blk)
            wq, _ = load("wq", [P, INNER], blk, 1)
            wk, _ = load("wk", [P, INNER], blk, 1)
            wv, _ = load("wv", [P, INNER], blk, 1)
            wg, _ = load("wg", [P, INNER], blk, 1)
            wo, _ = load("wo", [P, IC, P], blk, 1)
            esel, _ = load("esel", [P, IC, HEADS], blk, 1)
            mask, _ = load("mask", [P, QG], blk, 1)
            hv, _ = load("hv", [P, 2 * IC], blk, 1)
            mk, _ = load("mk", [HEADS * MEM, 2 * DH], blk, 1)
            w1 = load_ffn("f1", blk)
            w1_in = w1["in"]

            pre = sb1("pre", [P, P])
            post = sb1("post", [P, P])
            pre_zero = pool.do(lambda e: e.memset(pre[:], 0.0))
            post_zero = pool.do(lambda e: e.memset(post[:], 0.0))
            sp.wait(pre_zero, post_zero)
            mixes = Dma(sem("mixes_in"))
            for q in range(QG):
                s = slice(q * HEADS, (q + 1) * HEADS)
                mixes.start(sp, pre[s, s], d["preT"])
                mixes_in = mixes.start(sp, post[s, s], d["postT"])

            LO = HALF * W_LO
            T8 = sb1("T8", [P, LO + HALF * W_HI + 4 * (W_HI + QG)])

            def row(g):
                return g * W_LO if g < HALF else LO + (g - HALF) * W_HI

            def scores(g, a=0, z=None):
                z = seen_by(g) if z is None else z
                return T8[:, row(g) + a:row(g) + z]

            SN = sb1("SN", [P, HEADS, KEYS])
            qz = sb1("qz", [P, HEADS, SEQ])
            kT = sb1("kT", [P, IC, KEYS])
            ktok = sb1("ktok", [P, 2, INNER])
            sq = [sb1(f"sq{i}", [P, 512]) for i in range(2)]
            qn = sb1("qn", [HEADS, SEQ])
            rq = sb1("rq", [P, 2 * HEADS])
            rk = sb1("rk", [P, 2 * HEADS])
            V = sb1("V", [P, 3, INNER])
            gate = sb1("gate", [P, IC, SEQ])
            AT0 = sb1("AT0", [P, HEADS, SEQ])
            N1 = SEQ - (HALF - 1) * QG
            AT1 = sb1("AT1", [P, HEADS, N1])
            AT2 = sb1("AT2", [MEM, HEADS, QG])
            NXB = 3
            xb = [sb1(f"xb{i}", [P, MEM + SEQ]) for i in range(NXB)]
            x_slot = [Dma(sem(f"xb{i}")) for i in range(NXB)]
            NE = 4
            E = [sb1(f"E{i}", [P, KEYS]) for i in range(NE)]
            W = [sb1(f"W{i}", [P, KEYS]) for i in range(2)]
            neg = [sb1(f"neg{i}", [P, P]) for i in range(2)]
            posts = [sb1(f"posts{i}", [P, P]) for i in range(NE)]
            top = [sb1(f"top{i}", [P, 8]) for i in range(4)]
            peak = sb1("peak", [P, GROUPS])
            total = sb1("total", [P, GROUPS])
            share = sb1("share", [P, GROUPS])
            r2 = sb1("r2", [P, SEQ])
            x_c = sb1("x_c", [P, SEQ])
            r3 = sb1("r3", [P, SEQ])
            x_d = [sb1(f"x_d{i}", [P, SEQ]) for i in range(2)]
            y_slot = [Dma(sem(f"y_out{i}")) for i in range(2)]
            h1 = {"act": sb1("g_act", [P, 2, SEQ]), "a": sb1("g_a", [P, HC, SEQ]), "b": sb1("g_b", [P, HC, SEQ]), "free": ()}
            group_slot = [Dma(sem(f"group_in{i}")) for i in range(8)]
            memv_slot = Dma(sem("memv_in"))

            zeroed = [pool.do(lambda e, t=t: e.memset(t, 0.0)) for t in
                      (T8[:], qz[:].rearrange("p h t -> p (h t)"), AT1[:].rearrange("p h t -> p (h t)"),
                       *(x[:, 0:MEM] for x in xb))]

            KM = HEADS * MEM
            dve.wait(w1_in)
            act.wait(w1_in)
            mks = act.do(lambda e: e.activation(sq[0][0:KM, 0:DH], mk[:, 0:DH], ACT.Square))
            dve.wait(mks)
            mkr = dve.do(lambda e: e.tensor_reduce(rk[0:KM, 0:1], sq[0][0:KM, 0:DH], mybir.AxisListType.X, ALU.add))
            act.wait(mkr)
            mkr = act.do(lambda e: e.activation(rk[0:KM, 1:2], rk[0:KM, 0:1], ACT.Sqrt))
            dve.wait(mkr)
            mkr = dve.do(lambda e: e.tensor_scalar(rk[0:KM, 2:3], rk[0:KM, 1:2], NORM_EPS, None, ALU.max))
            dve.wait(mkr)
            mkr = dve.do(lambda e: e.reciprocal(rk[0:KM, 3:4], rk[0:KM, 2:3]))
            dve.wait(mkr)
            mkr = dve.do(lambda e: e.tensor_scalar(sq[1][0:KM, 0:P], mk[:], rk[0:KM, 3:4], None, ALU.mult))
            pe.wait(mkr)
            mkr = pe.do(lambda e: e.transpose(bank[0][:, 0:KM], sq[1][0:KM, 0:P], ident[0:KM, 0:KM]))
            dve.wait(mkr)
            for half in range(2):
                rows = slice(half * DH, (half + 1) * DH)
                src = bank[0][rows, 0:KM].rearrange("p (c two m) -> p c two m", two=2, m=MEM)[:, :, half, :]
                memk_ready = dve.do(lambda e, rows=rows, src=src: e.tensor_copy(kT[rows, :, 0:MEM], src))
            hh = sb1("hh", [P, 2 * IC])
            halved = dve.do(lambda e: e.tensor_scalar(hh[:], hv[:], 0.5, None, ALU.mult))
            dve.wait(halved)
            for c in range(IC):
                wo_ready = dve.do(lambda e, c=c: e.tensor_scalar(wo[:, c, :], wo[:, c, :], hh[:, c:c + 1], None, ALU.mult))

            banksA, banksD, banksT, banksC = Banks(bank[0:2]), Banks(bank[2:4]), Banks(bank[4:6]), Banks(bank[6:8])
            banksA.free(0, memk_ready)
            m = {}

            def once(key):
                while key not in m:
                    yield BLOCKED
                return m[key]

            def attention_front():
                for b in range(SEQS):
                    x = xb[b % NXB]
                    if b >= NXB:
                        sp.wait((yield from once(("x_used", b - NXB))))
                    loaded = x_slot[b % NXB].start(sp, x[:, MEM:], x_mid[:, b * SEQ:(b + 1) * SEQ])
                    pe.wait(loaded, w1_in, *zeroed)
                    q_sums, qsn = None, None
                    act.wait(zeroed[1])
                    for c2 in range(IC // 2):
                        o, n = banksA.take(pe)
                        for c in range(2):
                            at = (2 * c2 + c) * P
                            made = pe.do(matmul(o[:, c * SEQ:(c + 1) * SEQ], wq[:, at:at + P], x[:, MEM:]))
                        yield
                        s = sq[c2 % 2]
                        act.wait(made, *m.get(("sq_used", c2 % 2), ()))
                        squared = act.do(lambda e: e.activation(s[:], o[:], ACT.Square))
                        if b and c2 == 0:
                            act.wait(m["s_made", b - 1])
                        for half in range(2):
                            rows = slice(half * DH, (half + 1) * DH)
                            dst = qz[rows, 4 * c2:4 * c2 + 4, :].rearrange("p (c two) t -> p c two t", two=2)[:, :, half, :]
                            src = o[rows, :].rearrange("p (c t) -> p c t", c=2)
                            copied = act.do(lambda e, dst=dst, src=src: e.activation(dst, src, ACT.Copy))
                        banksA.free(n, copied)
                        pe.wait(squared)
                        if c2 == 0:
                            q_sums, qsn = banksD.take(pe)
                        for c in range(2):
                            cc = 2 * c2 + c
                            summed = pe.do(matmul(q_sums[0:HEADS, 0:SEQ], esel[:, cc, :], s[:, c * SEQ:(c + 1) * SEQ],
                                                  start=cc == 0, stop=cc == IC - 1))
                        m["sq_used", c2 % 2] = (summed,)
                        yield
                    act.wait(summed)
                    qn_made = act.do(lambda e: e.activation(qn[:], q_sums[0:HEADS, 0:SEQ], ACT.Copy))
                    banksD.free(qsn, qn_made)
                    yield
                    pe.wait(qn_made)
                    o, n = banksA.take(pe)
                    for t in range(2):
                        turned = pe.do(lambda e, t=t: e.transpose(o[:, t * HEADS:(t + 1) * HEADS], qn[:, t * P:(t + 1) * P],
                                                                  ident[0:HEADS, 0:HEADS]))
                    yield
                    act.wait(turned)
                    if b:
                        act.wait(m["sn_made", b - 1])
                    rooted = act.do(lambda e: e.activation(rq[:], o[:, 0:2 * HEADS], ACT.Sqrt))
                    banksA.free(n, rooted)
                    dve.wait(rooted)
                    rooted = dve.do(lambda e: e.tensor_scalar(rq[:], rq[:], NORM_EPS, 1.0 / QK_SCALE, ALU.max, ALU.mult))
                    dve.wait(rooted)
                    rq_ready = dve.do(lambda e: e.reciprocal(rq[:], rq[:]))
                    yield
                    for t in range(2):
                        norm = rk[:, t * HEADS:(t + 1) * HEADS]
                        halves = []
                        for f in range(2):
                            o, n = banksA.take(pe)
                            made = pe.do(matmul(o[:], x[:, MEM + t * P:MEM + (t + 1) * P], wk[:, f * 512:(f + 1) * 512]))
                            s = sq[f]
                            act.wait(made, *m.get(("sq_used", f), ()))
                            squared = act.do(lambda e, s=s, o=o: e.activation(s[:], o[:], ACT.Square))
                            yield
                            dve.wait(squared)
                            reduced = dve.do(lambda e, s=s, f=f: e.tensor_reduce(
                                norm[:, f * 8:(f + 1) * 8], s[:].rearrange("p (h d) -> p h d", d=DH), mybir.AxisListType.X, ALU.add))
                            m["sq_used", f] = (reduced,)
                            halves.append((o, n, made))
                            yield
                        act.wait(reduced)
                        rooted = act.do(lambda e: e.activation(norm, norm, ACT.Sqrt))
                        yield
                        dve.wait(rooted)
                        rooted = dve.do(lambda e: e.tensor_scalar(norm, norm, NORM_EPS, None, ALU.max))
                        dve.wait(rooted)
                        rooted = dve.do(lambda e: e.reciprocal(norm, norm))
                        dve.wait(rooted)
                        if b:
                            dve.wait(m["k_turned", b - 1])
                        for f, (o, n, made) in enumerate(halves):
                            dst = ktok[:, t, f * 512:(f + 1) * 512].rearrange("p (h d) -> p h d", d=DH)
                            src = o[:].rearrange("p (h d) -> p h d", d=DH)
                            nrm = norm[:, f * 8:(f + 1) * 8].unsqueeze(2).to_broadcast([P, 8, DH])
                            scaled = dve.do(lambda e, dst=dst, src=src, nrm=nrm: e.tensor_tensor(dst, src, nrm, ALU.mult))
                            banksA.free(n, scaled)
                        yield
                        pe.wait(scaled)
                        for c4 in range(2):
                            o, n = banksA.take(pe)
                            for c in range(4):
                                at = (4 * c4 + c) * P
                                turned = pe.do(lambda e, o=o, c=c, at=at, t=t: e.transpose(
                                    o[:, c * P:(c + 1) * P], ktok[:, t, at:at + P], ident[:]))
                            act.wait(turned)
                            if b:
                                act.wait(m["s_made", b - 1])
                            k_ready = act.do(lambda e, o=o, c4=c4, t=t: e.activation(
                                kT[:, 4 * c4:4 * c4 + 4, MEM + t * P:MEM + (t + 1) * P],
                                o[:].rearrange("p (c t) -> p c t", c=4), ACT.Copy))
                            banksA.free(n, k_ready)
                            yield
                    m["k_turned", b] = turned
                    for blk_q in range(2):
                        width = W_LO if blk_q == 0 else W_HI
                        per = 3 if blk_q == 0 else 1
                        pe.wait(k_ready, copied, memk_ready)
                        for h0_ in range(0, HEADS, per):
                            hs_ = range(h0_, min(h0_ + per, HEADS))
                            o, n = banksA.take(pe)
                            for j, h in enumerate(hs_):
                                made = pe.do(matmul(o[:, j * width:(j + 1) * width], qz[:, h, blk_q * P:(blk_q + 1) * P],
                                                    kT[:, h // 2, 0:width]))
                            act.wait(made, rq_ready)
                            if h0_ == 0 and ("sn_sent", b, blk_q) != ("sn_sent", 0, 0):
                                act.wait(*m["sn_sent"])
                            for j, h in enumerate(hs_):
                                c = blk_q * HEADS + h
                                evac = act.do(lambda e, o=o, j=j, h=h, c=c: e.activation(
                                    SN[:, h, 0:width], o[:, j * width:(j + 1) * width], ACT.Copy, scale=rq[:, c:c + 1]))
                            banksA.free(n, evac)
                            yield
                        m["sn_made", b] = evac
                        if blk_q == 1:
                            m["s_made", b] = made
                        sp.wait(evac)
                        m["sn_sent"] = []
                        queued = []
                        for step in range(HALF + 2):
                            if step < HALF:
                                g = blk_q * HALF + step
                                if b:
                                    sp.wait((yield from once(("mixed_back", b - 1, g))))
                                elif g == 0:
                                    sp.wait(zeroed[0])
                                slot = group_slot[g % 8]
                                sp.wait(*m.get(("slot_read", g % 8), ()))
                                sent = slot.start(sp, scores(g), SN[step * QG:(step + 1) * QG, :, 0:seen_by(g)])
                                m["sn_sent"].append(sent)
                                queued.append((g, sent))
                            if step >= 2:
                                g, sent = queued[step - 2]
                                pe.wait(sent, mixes_in)
                                o, n = banksD.take(pe)
                                mixed = pe.do(matmul(o[:, 0:seen_by(g)], pre[:], scores(g)))
                                m["slot_read", g % 8] = (mixed,)
                                act.wait(mixed)
                                stored = act.do(lambda e, o=o, g=g: e.activation(scores(g), o[:, 0:seen_by(g)], ACT.Copy))
                                banksD.free(n, stored)
                                if g % 4 == 3:
                                    g0 = g - 3
                                    stride = (W_LO if g < HALF else W_HI) + QG
                                    at = row(g0) + seen_by(g0) - QG
                                    tri = T8[:, at:at + 4 * stride].rearrange("p (g x) -> p g x", x=stride)[:, :, 0:QG]
                                    dve.wait(stored)
                                    masked = dve.do(lambda e, tri=tri: e.tensor_tensor(
                                        tri, tri, mask[:].unsqueeze(1).to_broadcast([P, 4, QG]), ALU.add))
                                    for k in range(4):
                                        m["scores", b, g0 + k] = masked
                            yield
                    yield DONE

            def top_k():
                e_used = [None] * NE
                w_used = [None] * 2
                for b in range(SEQS):
                    def rank(g, k_top, b=b):
                        n_keys, s, first, j = seen_by(g), scores(g), top[k_top], g % NE
                        if b:
                            dve.wait(m["peak_read", b - 1])
                        dve.wait(m["scores", b, g])
                        best = dve.do(lambda e: e.max(first[:], s))
                        yield
                        dve.wait(best)
                        peaked = dve.do(lambda e: e.tensor_scalar(peak[:, g:g + 1], first[:, 0:1], -1.0, None, ALU.mult))
                        yield
                        if n_keys <= TOPK:
                            act.wait(peaked)
                            summed = act.do(lambda e: e.activation(s, s, ACT.Exp, bias=peak[:, g:g + 1],
                                                                   accum_out=total[:, g:g + 1]))
                        else:
                            act.wait(peaked, *([e_used[j]] if e_used[j] else []))
                            exped = act.do(lambda e: e.activation(E[j][:, 0:n_keys], s, ACT.Exp, bias=peak[:, g:g + 1]))
                            below = n_keys - TOPK + 1
                            turn = below < TOPK
                            nth = below if turn else TOPK
                            base = s
                            if turn:
                                nt = neg[g % 2]
                                pool.wait(m["scores", b, g], *([w_used[g % 2]] if w_used[g % 2] else []))
                                turned = pool.do(lambda e: e.tensor_scalar(nt[:, 0:n_keys], s, -1.0, 1.0, ALU.mult, ALU.mult))
                                base = nt[:, 0:n_keys]
                                dve.wait(turned, peaked)
                                best = dve.do(lambda e: e.max(first[:], base))
                                yield
                            work = W[g % 2][:, 0:n_keys]
                            src = base
                            for _ in range((nth - 1) // 8):
                                dve.wait(best)
                                cut = dve.do(lambda e: e.match_replace(work, first[:], src, MASKED))
                                yield
                                dve.wait(cut)
                                best = dve.do(lambda e: e.max(first[:], work))
                                src = work
                                yield
                            at = (nth - 1) % 8
                            dve.wait(best, exped)
                            summed = dve.do(lambda e: e.scalar_tensor_tensor(
                                out=s, in0=base, scalar=first[:, at:at + 1], in1=E[j][:, 0:n_keys],
                                op0=ALU.is_le if turn else ALU.is_ge, op1=ALU.mult, accum_out=total[:, g:g + 1]))
                            e_used[j] = summed
                            w_used[g % 2] = summed
                            yield
                        dve.wait(summed)
                        m["peak_read", b] = summed
                        m["share", b, g] = dve.do(lambda e: e.reciprocal(share[:, g:g + 1], total[:, g:g + 1]))

                    for g in range(0, GROUPS, 2):
                        for k in (g, g + 1):
                            yield from once(("scores", b, k))
                        pair = [rank(g, 0), rank(g + 1, 1)]
                        while pair:
                            pair = [r for r in pair if next(r, "ended") != "ended"]
                            yield 2 * (seen_by(g) + 90) / 1000
                    yield DONE

            def mix_turned():
                p_used = [None] * NE
                for b in range(SEQS):
                    def mix_back(g, ready, b=b):
                        j = g % NE
                        pool.wait(ready, *([p_used[j]] if p_used[j] else []))
                        scaled = pool.do(lambda e: e.tensor_scalar(posts[j][:], post[:], share[:, g:g + 1], 1.0, ALU.mult, ALU.mult))
                        pe.wait(scaled, mixes_in)
                        if g % 4 == 0:
                            m["at0"] = banksT.take(pe)
                        o0, n0 = m["at0"]
                        turned = pe.do(matmul(o0[:, (g % 4) * P:(g % 4 + 1) * P], scores(g, 0, P), posts[j][:]))
                        if g >= HALF:
                            if g % 4 == 0:
                                m["at1"] = banksT.take(pe)
                            o1, n1 = m["at1"]
                            turned = pe.do(matmul(o1[:, (g % 4) * P:(g % 4 + 1) * P], scores(g, P, 2 * P), posts[j][:]))
                        if g in (HALF - 1, GROUPS - 1):
                            o, n = banksD.take(pe)
                            a = P if g == HALF - 1 else 2 * P
                            turned = pe.do(matmul(o[0:MEM, 0:P], scores(g, a, a + MEM), posts[j][:]))
                            dst = AT1[0:MEM, :, 0:QG] if g == HALF - 1 else AT2[:]
                            src = o[0:MEM, 0:P].rearrange("p (q h) -> p h q", h=HEADS)
                            act.wait(turned)
                            if b:
                                act.wait(m["at_read", b - 1])
                            banksD.free(n, act.do(lambda e: e.activation(dst, src, ACT.Copy)))
                        m["mixed_back", b, g] = turned
                        p_used[j] = turned
                        return turned

                    def drain(g, turned, b=b):
                        if g % 4 != 3:
                            return
                        act.wait(turned)
                        if b:
                            act.wait(m["at_read", b - 1])
                        o0, n0 = m["at0"]
                        q0 = (g - 3) * QG
                        src = o0[:].rearrange("p (q h) -> p h q", h=HEADS)
                        done = act.do(lambda e: e.activation(AT0[:, :, q0:q0 + 4 * QG], src, ACT.Copy))
                        banksT.free(n0, done)
                        if g >= HALF:
                            o1, n1 = m["at1"]
                            q1 = q0 - (HALF - 1) * QG
                            src1 = o1[:].rearrange("p (q h) -> p h q", h=HEADS)
                            done = act.do(lambda e: e.activation(AT1[:, :, q1:q1 + 4 * QG], src1, ACT.Copy))
                            banksT.free(n1, done)
                        if g == GROUPS - 1:
                            m["at", b] = done

                    turned = {}
                    for g in range(GROUPS + 1):
                        if g % 4 == 0 and g:
                            if b:
                                yield from once(("at_read", b - 1))
                            drain(g - 1, turned[g - 1])
                        if g < GROUPS:
                            yield from once(("share", b, g))
                            turned[g] = mix_back(g, m["share", b, g])
                        yield
                    yield DONE

            def attention_back():
                for b in range(SEQS):
                    x = xb[b % NXB]
                    yield from once(("s_made", b))
                    for t, size in ((0, P), (1, P), (2, MEM)):
                        for f in range(2):
                            o, n = banksC.take(pe)
                            made = pe.do(matmul(o[0:size, :], x[:, t * P:t * P + size], wv[:, f * 512:(f + 1) * 512]))
                            yield
                            act.wait(made)
                            if b:
                                act.wait(m["at_read", b - 1])
                            v_made = act.do(lambda e, o=o, t=t, f=f, size=size: e.activation(
                                V[0:size, t, f * 512:(f + 1) * 512], o[0:size, :], ACT.Copy))
                            banksC.free(n, v_made)
                            yield
                        if t == 0:
                            sp.wait(v_made)
                            memv_ready = memv_slot.start(sp, V[0:MEM, 0, :], d["mem_v"])
                    for c2 in range(IC // 2):
                        o, n = banksC.take(pe)
                        for c in range(2):
                            at = (2 * c2 + c) * P
                            made = pe.do(matmul(o[:, c * SEQ:(c + 1) * SEQ], wg[:, at:at + P], x[:, MEM:]))
                        yield
                        act.wait(made, halved)
                        if b:
                            act.wait(m["ctx_read", b - 1])
                        for c in range(2):
                            cc = 2 * c2 + c
                            gate_ready = act.do(lambda e, o=o, c=c, cc=cc: e.activation(
                                gate[:, cc, :], o[:, c * SEQ:(c + 1) * SEQ], ACT.Tanh, bias=hh[:, IC + cc:IC + cc + 1], scale=0.5))
                        banksC.free(n, gate_ready)
                        yield
                    at_ready = yield from once(("at", b))
                    pe.wait(at_ready, v_made, memv_ready)
                    for c2 in range(IC // 2):
                        o, n = banksC.take(pe)
                        for c in range(2):
                            for half in range(2):
                                cc = 2 * c2 + c
                                h = 2 * cc + half
                                out_ = o[half * DH:(half + 1) * DH, c * SEQ:(c + 1) * SEQ]
                                cols = slice(h * DH, (h + 1) * DH)
                                pe.quiet(matmul(out_, V[:, 0, cols], AT0[:, h, :], start=True, stop=False))
                                pe.quiet(matmul(out_[:, SEQ - N1:SEQ], V[:, 1, cols], AT1[:, h, :], start=False, stop=False))
                                made = pe.do(matmul(out_[:, SEQ - QG:SEQ], V[0:MEM, 2, cols], AT2[:, h, :], start=False, stop=True))
                        m["at_read", b] = made
                        yield
                        dve.wait(made, gate_ready)
                        view = gate[:, 2 * c2:2 * c2 + 2, :].rearrange("p c t -> p (c t)")
                        gated = dve.do(lambda e, o=o, view=view: e.scalar_tensor_tensor(
                            out=view, in0=view, scalar=1.0, in1=o[:], op0=ALU.add, op1=ALU.mult))
                        banksC.free(n, gated)
                        yield
                    pe.wait(gated, wo_ready)
                    o, n = banksC.take(pe)
                    for c in range(IC):
                        step = matmul(o[:, 0:SEQ], wo[:, c, :], gate[:, c, :], start=c == 0, stop=c == IC - 1)
                        if c < IC - 1:
                            pe.quiet(step)
                        else:
                            made = pe.do(step)
                    m["ctx_read", b] = made
                    yield
                    dve.wait(made)
                    added = dve.do(lambda e, o=o: e.tensor_tensor(r2[:], o[:, 0:SEQ], x[:, MEM:], ALU.add))
                    banksC.free(n, added)
                    m["x_used", b] = added
                    x_c_ready = yield from layer_norm(r2[:], added, 0, banksC, x_c[:])
                    yield
                    added = yield from ffn(w1, h1, x_c[:], x_c_ready, banksC, (), r3[:])
                    free = (m["y", b - 2],) if b >= 2 else ()
                    normed = yield from layer_norm(r3[:], added, 1, banksC, x_d[b % 2][:], free)
                    sp.wait(normed)
                    m["y", b] = y_slot[b % 2].start(sp, out[:, b * SEQ:(b + 1) * SEQ], x_d[b % 2][:])
                    yield DONE

            interleave([(attention_front(), 85, -1), (top_k(), 115, 0), (mix_turned(), 33, 0), (attention_back(), 60, 0.6)])
            sp.wait(m["y", SEQS - 2], m["y", SEQS - 1])


def lay_out(i):
    a = {}
    as_is = lambda x: np.ascontiguousarray(np.asarray(x))
    a["xT"] = as_is(np.asarray(i["L0_attn_x"]).reshape(SEQS * SEQ, P).T)
    w_in = np.asarray(i["L0_attn_W_in"])
    a["w_in"], a["w_resT"] = as_is(w_in[:P]), as_is(w_in[P:].T)
    a["w_dtT"], a["w_outT"] = as_is(np.asarray(i["L0_attn_W_dt"]).T), as_is(np.asarray(i["L0_attn_W_out"]).T)
    col = lambda n: np.asarray(i[n]).reshape(-1, 1)
    a["vec"] = np.concatenate([np.asarray(i["L0_attn_conv_w"]), col("L0_attn_conv_b"), col("L0_attn_b_dt"), col("L0_attn_Dp")], 1)
    a["ssm"] = np.concatenate([np.asarray(i[f"L0_attn_{n}"]) for n in ("A_log", "Bp", "Cp")], 1)
    by_chunk = lambda x: np.asarray(x).reshape(-1, P).T
    for b in (0, 1):
        f = lambda n: np.asarray(i[f"L{b}_ffn_{n}"])
        a[f"f{b}w1"], a[f"f{b}w2"] = as_is(f("w1_w").T), as_is(f("w2_w").T)
        for n in ("h1", "h2"):
            a[f"f{b}{n}"] = as_is(f(n + "_w").T.reshape(HC, P, HID).transpose(1, 0, 2))
        a[f"f{b}w3"] = as_is(f("w3_w").T.reshape(HC, P, P).transpose(1, 0, 2))
        a[f"f{b}s"] = np.concatenate([by_chunk(f(n + "_s")) for n in ("w1", "w2", "h1", "h2", "w3")], 1)
    g = lambda n: np.asarray(i[f"L1_attn_{n}"])
    for n in ("q", "k", "v", "g"):
        a["w" + n] = as_is(g("W" + n))
    a["wo"] = as_is(g("Wo").reshape(IC, P, P).transpose(1, 0, 2))
    a["preT"], a["postT"] = as_is(g("W_pre_th").T), as_is(g("W_post_th").T)
    mk = g("mem_k").reshape(HEADS * MEM, DH)
    a["mk"] = np.concatenate([mk, mk], 1)
    a["mem_v"] = as_is(g("mem_v").transpose(1, 0, 2).reshape(MEM, INNER))
    scale = np.broadcast_to(g("head_scale_params").reshape(HEADS, 1), (HEADS, DH))
    a["hv"] = np.concatenate([by_chunk(as_is(scale)), by_chunk(g("bg"))], 1)
    a["ident"] = np.eye(P, dtype=np.float32)
    a["meanmat"] = np.full((P, P), 1.0 / P, np.float32)
    esel = np.zeros((P, IC, HEADS), np.float32)
    for c in range(IC):
        esel[:DH, c, 2 * c] = 1.0
        esel[DH:, c, 2 * c + 1] = 1.0
    a["esel"] = esel
    query = np.arange(P)[:, None] // HEADS
    a["mask"] = np.where(np.arange(QG)[None, :] > query, np.float32(MASKED), np.float32(0.0)).astype(np.float32)
    return {n: np.ascontiguousarray(x) for n, x in a.items()}


def kernel(**inputs):
    import concourse.bacc as bacc
    from concourse.bass_utils import run_bass_kernel_spmd

    nc = bacc.Bacc("TRN2", target_bir_lowering=False, num_devices=1)
    arrays = lay_out(inputs)
    d = {n: nc.dram_tensor("in_" + n, a.shape, mybir.dt.from_np(a.dtype), kind="ExternalInput").ap()
         for n, a in arrays.items()}
    out = nc.dram_tensor("out_y", [P, SEQS * SEQ], F32, kind="ExternalOutput").ap()
    program(nc, d, out)
    r = run_bass_kernel_spmd(nc, [{"in_" + n: a for n, a in arrays.items()}], core_ids=[0])
    y = np.asarray(r.results[0]["out_y"])
    return np.ascontiguousarray(y.T).reshape(SEQS, SEQ, P)
```

```python
from contextlib import ExitStack

import numpy as np

import concourse.bass as bass
from concourse import mybir

F32 = mybir.dt.float32
ALU = mybir.AluOpType
ACT = mybir.ActivationFunctionType

P = 128
SEQS, SEQ = 32, 256
STATES, TAPS = 16, 4
HID = 512
HC = HID // P
HEADS, DH, MEM, TOPK = 16, 64, 4, 64
INNER = HEADS * DH
IC = INNER // P
KEYS = MEM + SEQ
QG = P // HEADS
GROUPS = SEQ // QG
QK_SCALE = 10.0
LN_EPS = 1e-5
NORM_EPS = 1e-12
MASKED = float(np.finfo(np.float32).min)
HALF = GROUPS // 2
W_LO, W_HI = MEM + P, KEYS


def seen_by(group):
    return MEM + QG * (group + 1)


SIGNAL = 0.1


class Plan:
    done = {}
    latest = 0.0


class Engine:

    def __init__(self, engine, sem, fixed, column):
        self.engine, self.sem, self.count, self.waited = engine, sem, 0, {}
        self.fixed, self.column, self.clock = fixed, column, 0.0

    def wait(self, *marks):
        for sem, value in marks:
            if self.waited.get(sem.name, 0) < value:
                self.waited[sem.name] = value
                self.engine.wait_ge(sem, value)
                self.clock = max(self.clock, Plan.done[sem.name, value] + SIGNAL)

    def do(self, step, columns=SEQ):
        self.count += 1
        step(self.engine).then_inc(self.sem, 1)
        self.clock += self.fixed + self.column * columns
        Plan.done[self.sem.name, self.count] = Plan.latest = self.clock
        return (self.sem, self.count)

    def quiet(self, step, columns=SEQ):
        step(self.engine)
        self.clock += self.fixed + self.column * columns


class Activations(Engine):
    loaded = None

    def tables(self, name):
        if self.loaded != name:
            self.loaded = name
            self.engine.preload_act_table_set(name)
            self.clock += TABLE_LOAD


EXP_LN, SILU, GELU = "natural_log_exp_and_others", "silu_and_others", "gelu_and_others"
TABLE_LOAD = 1.3


class Dma:

    def __init__(self, sem):
        self.sem, self.count = sem, 0

    def start(self, queue, out, in_):
        self.count += 16
        queue.engine.dma_start(out, in_).then_inc(self.sem, 16)
        queue.clock += 0.1
        Plan.done[self.sem.name, self.count] = queue.clock + 2.0
        return (self.sem, self.count)


class Banks:
    TAKEN = "taken"

    def __init__(self, banks):
        self.banks, self.freed = banks, [None] * len(banks)

    def first_free(self):
        return min(((Plan.done[f[0].name, f[1]] if f else 0.0, n) for n, f in enumerate(self.freed)
                    if f is not Banks.TAKEN), default=None)

    def take(self, engine):
        while self.first_free() is None:
            yield BLOCKED
        yield self.first_free()[0]
        while self.first_free() is None:
            yield BLOCKED
        n = self.first_free()[1]
        if self.freed[n]:
            engine.wait(self.freed[n])
        self.freed[n] = Banks.TAKEN
        return self.banks[n], n

    def free(self, n, mark):
        self.freed[n] = mark


BLOCKED = "blocked"


def interleave(actors):
    live = [[gen, 0.0] for gen in actors]
    stuck = []
    while live:
        ready = [a for a in live if a[0] not in stuck]
        if not ready:
            raise AssertionError("every actor is blocked")
        a = min(ready, key=lambda a: a[1])
        Plan.latest = 0.0
        said = next(a[0], "ended")
        if said == BLOCKED:
            stuck.append(a[0])
            continue
        stuck = []
        if said == "ended":
            live.remove(a)
        else:
            a[1] = max(a[1], Plan.latest, said or 0.0)


def once(marks, key):
    while key not in marks:
        yield BLOCKED
    sem, value = marks[key]
    yield Plan.done[sem.name, value]
    return marks[key]


def program(nc, d, out):
    with ExitStack() as ctx:
        n_sem = [0]

        def sem(name):
            n_sem[0] += 1
            return ctx.enter_context(nc.semaphore(name))

        def sb(name, shape, dt=F32, scope=ctx):
            return scope.enter_context(nc.sbuf_tensor(name, shape, dt))

        pe, act = Engine(nc.tensor, sem("pe_done"), 0.1, 0.0012), Activations(nc.scalar, sem("act_done"), 0.2, 0.00083)
        dve, pool = Engine(nc.vector, sem("dve_done"), 0.1, 0.00104), Engine(nc.gpsimd, sem("pool_done"), 0.1, 0.002)
        sp = Engine(nc.sync, sem("sp_done"), 0.1, 0.0)
        bank = [ctx.enter_context(nc.psum_tensor(f"bank{i}", [P, 512], F32)) for i in range(8)]
        x_mid = nc.dram_tensor("x_mid", [P, SEQS * SEQ], F32).ap()

        def matmul(o, l, r, start=True, stop=True):
            return lambda e: e.matmul(o, l, r, start=start, stop=stop)

        weights = {0: Dma(sem("weights0_in")), 1: Dma(sem("weights1_in"))}

        def load(name, shape, scope=ctx, block=0):
            t = sb("w_" + name, shape, scope=scope)
            return t, weights[block].start(sp, t[:], d[name])

        ident, _ = load("ident", [P, P])
        meanmat, consts_in = load("meanmat", [P, P])

        ln_cen = [sb(f"ln_cen{i}", [P, SEQ]) for i in range(2)]
        ln_sq = [sb(f"ln_sq{i}", [P, SEQ]) for i in range(2)]
        ln_var = [sb(f"ln_var{i}", [P, 2]) for i in range(2)]
        ln_t = [sb(f"ln_t{i}", [P, 2]) for i in range(2)]
        ln_rs = [sb(f"ln_rs{i}", [P, 2]) for i in range(2)]

        def inverse_root(v, v_ready, y, t):
            n = v.shape[-1]
            act.wait(v_ready)
            act.tables(EXP_LN)
            logged = act.do(lambda e: e.activation(t, v, ACT.Ln), n)
            act.wait(logged)
            rooted = act.do(lambda e: e.activation(y, t, ACT.Exp, scale=-0.5), n)
            yield
            for step in (lambda e: e.tensor_tensor(t, y, y, ALU.mult), lambda e: e.tensor_tensor(t, t, v, ALU.mult),
                         lambda e: e.tensor_scalar(t, t, -0.5, 1.5, ALU.mult, ALU.add),
                         lambda e: e.tensor_tensor(y, y, t, ALU.mult)):
                pool.wait(rooted)
                rooted = pool.do(step, n)
            yield
            return rooted

        def layer_norm(r, r_ready, slot, banks, result, result_free=()):
            cen, sq, sd, rs, scratch = ln_cen[slot], ln_sq[slot], ln_var[slot], ln_rs[slot], ln_t[slot]
            pe.wait(r_ready)
            mean, n = yield from banks.take(pe)
            meaned = pe.do(matmul(mean[:, 0:SEQ], meanmat[:], r))
            yield
            dve.wait(meaned)
            centred = dve.do(lambda e: e.tensor_tensor(cen[:], r, mean[:, 0:SEQ], ALU.subtract))
            banks.free(n, centred)
            act.wait(centred)
            squared = act.do(lambda e: e.activation(sq[:], cen[:], ACT.Square))
            yield
            pe.wait(squared)
            var, n = yield from banks.take(pe)
            for t in range(2):
                step = matmul(var[:, t:t + 1], sq[:, t * P:(t + 1) * P], meanmat[:, 0:1])
                varied = pe.do(step)
            yield
            dve.wait(varied)
            lifted = dve.do(lambda e: e.tensor_scalar(sd[:], var[:, 0:2], LN_EPS, None, ALU.add), 2)
            banks.free(n, lifted)
            inverted = yield from inverse_root(sd[:], lifted, rs[:], scratch[:])
            pe.wait(inverted)
            spread, n = yield from banks.take(pe)
            for t in range(2):
                step = matmul(spread[:, t * P:(t + 1) * P], rs[:, t:t + 1].to_broadcast([P, P]), ident[:])
                spreaded = pe.do(step)
            yield
            dve.wait(spreaded, *result_free)
            normed = dve.do(lambda e: e.tensor_tensor(result, cen[:], spread[:, 0:SEQ], ALU.mult))
            banks.free(n, normed)
            return normed

        def load_ffn(b, scope):
            w, block = {}, int(b[1])
            w["w1"], _ = load(f"{b}w1", [P, HID], scope, block)
            w["w2"], _ = load(f"{b}w2", [P, HID], scope, block)
            for k in ("h1", "h2"):
                w[k], _ = load(b + k, [P, HC, HID], scope, block)
            w["w3"], _ = load(f"{b}w3", [P, HC, P], scope, block)
            w["s"], w["in"] = load(f"{b}s", [P, 4 * HC + 1], scope, block)
            return w

        def ffn(w, h, x, x_ready, banks, r_free, r):
            scale = lambda k, m: w["s"][:, k * HC + m:k * HC + m + 1]
            pe.wait(x_ready, w["in"])
            for k, layer in enumerate(("w1", "w2")):
                halves = []
                for m2 in range(HC // 2):
                    o, n = yield from banks.take(pe)
                    for m in range(2):
                        c = (2 * m2 + m) * P
                        made = pe.do(matmul(o[:, m * SEQ:(m + 1) * SEQ], w[layer][:, c:c + P], x))
                    halves.append((o, n, made))
                    yield
                if k == 0:
                    act.wait(made, *h["free"])
                    act.tables(SILU)
                    for m2, (o, n, _) in enumerate(halves):
                        for m in range(2):
                            ready = act.do(lambda e, m=m: e.activation(h["a"][:, 2 * m2 + m, :], o[:, m * SEQ:(m + 1) * SEQ],
                                                                       ACT.Silu, scale=scale(0, 2 * m2 + m)))
                        banks.free(n, ready)
                    yield
                else:
                    for m2, (o, n, made) in enumerate(halves):
                        dve.wait(ready, made)
                        for m in range(2):
                            hid = h["a"][:, 2 * m2 + m, :]
                            gated = dve.do(lambda e, m=m: e.scalar_tensor_tensor(
                                out=hid, in0=o[:, m * SEQ:(m + 1) * SEQ], scalar=scale(1, 2 * m2 + m), in1=hid,
                                op0=ALU.mult, op1=ALU.mult))
                        banks.free(n, gated)
                        yield
            src, ready = h["a"], gated
            for k, layer, dst in ((2, "h1", h["b"]), (3, "h2", h["a"])):
                pe.wait(ready)
                halves = []
                for m2 in range(HC // 2):
                    o, n = yield from banks.take(pe)
                    for m in range(2):
                        for c in range(HC):
                            step = matmul(o[:, m * SEQ:(m + 1) * SEQ], w[layer][:, c, (2 * m2 + m) * P:(2 * m2 + m + 1) * P],
                                          src[:, c, :], start=c == 0, stop=c == HC - 1)
                            if c < HC - 1:
                                pe.quiet(step)
                            else:
                                made = pe.do(step)
                        yield
                    halves.append((o, n))
                act.wait(made)
                act.tables(GELU)
                for m2, (o, n) in enumerate(halves):
                    for m in range(2):
                        ready = act.do(lambda e, m=m: e.activation(dst[:, 2 * m2 + m, :], o[:, m * SEQ:(m + 1) * SEQ],
                                                                   ACT.Gelu, scale=scale(k, 2 * m2 + m)))
                    banks.free(n, ready)
                yield
                src = dst
            pe.wait(ready)
            o, n = yield from banks.take(pe)
            for c in range(HC):
                step = matmul(o[:, 0:SEQ], w["w3"][:, c, :], src[:, c, :], start=c == 0, stop=c == HC - 1)
                if c < HC - 1:
                    pe.quiet(step)
                else:
                    made = pe.do(step)
            h["free"] = (made,)
            yield
            dve.wait(made, *r_free)
            added = dve.do(lambda e: e.scalar_tensor_tensor(out=r, in0=o[:, 0:SEQ], scalar=w["s"][:, 4 * HC:4 * HC + 1],
                                                            in1=x, op0=ALU.mult, op1=ALU.add))
            banks.free(n, added)
            return added

        with ExitStack() as blk:
            sb0 = lambda name, shape: sb(name, shape, scope=blk)
            w_in, _ = load("w_in", [P, P], scope=blk)
            w_res, _ = load("w_resT", [P, P], scope=blk)
            w_dt, _ = load("w_dtT", [P, P], scope=blk)
            w_out, _ = load("w_outT", [P, P], scope=blk)
            vec, _ = load("vec", [P, 7], scope=blk)
            ssm, _ = load("ssm", [P, 3 * STATES], scope=blk)
            w0 = load_ffn("f0", blk)
            w0_in = w0["in"]
            conv_b, b_dt, Dp = vec[:, 4:5], vec[:, 5:6], vec[:, 6:7]

            conv_d = sb0("conv_d", [P, TAPS, P])
            w_conv = sb0("w_conv", [P, TAPS, P])
            neg_a = sb0("neg_a", [P, STATES])
            bc = sb0("bc", [P, STATES])
            mix_d = sb0("mix_d", [P, STATES + 1, P])
            dve.wait(w0_in)
            for k in range(TAPS):
                tapped = dve.do(lambda e, k=k: e.tensor_scalar(conv_d[:, k, :], ident[:], vec[:, k:k + 1], None, ALU.mult))
            pe.wait(tapped)
            for k in range(TAPS):
                step = matmul(bank[0][:, k * P:(k + 1) * P], w_in[:], conv_d[:, k, :])
                folded = pe.do(step)
            dve.wait(folded)
            conv_ready = dve.do(lambda e: e.tensor_copy(w_conv[:].rearrange("p k n -> p (k n)"), bank[0][:]))
            act.wait(w0_in)
            act.tables(EXP_LN)
            a_made = act.do(lambda e: e.activation(neg_a[:], ssm[:, 0:STATES], ACT.Exp))
            dve.wait(a_made)
            a_ready = dve.do(lambda e: e.tensor_scalar(neg_a[:], neg_a[:], -1.0, None, ALU.mult))
            bc_made = dve.do(lambda e: e.tensor_tensor(bc[:], ssm[:, STATES:2 * STATES], ssm[:, 2 * STATES:3 * STATES], ALU.mult))
            dve.wait(bc_made)
            for s in range(STATES):
                dve.do(lambda e, s=s: e.tensor_scalar(mix_d[:, s, :], ident[:], bc[:, s:s + 1], None, ALU.mult))
            mix_ready = dve.do(lambda e: e.tensor_scalar(mix_d[:, STATES, :], ident[:], Dp, None, ALU.mult))

            NX = 4
            x_in = [sb0(f"x_in{i}", [P, 4 + SEQ]) for i in range(NX)]
            x_slot = [Dma(sem(f"x_in{i}")) for i in range(NX)]
            xc = [sb0(f"xc{i}", [P, SEQ]) for i in range(NX)]
            sres = [sb0(f"sres{i}", [P, SEQ]) for i in range(NX)]
            delta = [sb0(f"delta{i}", [P, SEQ]) for i in range(NX)]
            dx = [sb0(f"dx{i}", [P, SEQ]) for i in range(NX)]
            sp_t = [sb0(f"sp_t{i}", [P, SEQ]) for i in range(5)]
            ND = 4
            dA = [sb0(f"dA{i}", [P, SEQ]) for i in range(ND)]
            hs = [sb0(f"hs{i}", [P, SEQ]) for i in range(ND)]
            z = [sb0(f"z{i}", [P, SEQ]) for i in range(2)]
            r0 = [sb0(f"r0_{i}", [P, SEQ]) for i in range(2)]
            x_a = [sb0(f"x_a{i}", [P, SEQ]) for i in range(2)]
            r1 = [sb0(f"r1_{i}", [P, SEQ]) for i in range(2)]
            x_b = [sb0(f"x_b{i}", [P, SEQ]) for i in range(2)]
            out_slot = [Dma(sem(f"mid_out{i}")) for i in range(2)]
            h0 = [{"a": sb0(f"h_a{i}", [P, HC, SEQ]), "b": sb0(f"h_b{i}", [P, HC, SEQ]), "free": ()} for i in range(2)]

            pads = [pool.do(lambda e, t=t: e.memset(t[:, 0:4], 0.0)) for t in x_in]
            banks = Banks(bank)
            banks.free(0, conv_ready)
            m = {}

            def mixer_front():
                for b in range(SEQS):
                    i = b % NX
                    xt = x_in[i]
                    if b >= NX:
                        yield from once(m, ("x_used", b - NX))
                        sp.wait(m["x_used", b - NX])
                    loaded = x_slot[i].start(sp, xt[:, 4:], d["xT"][:, b * SEQ:(b + 1) * SEQ])
                    pe.wait(loaded, conv_ready, pads[i], w0_in)
                    conv, cn = yield from banks.take(pe)
                    for k in range(TAPS):
                        step = matmul(conv[:, 0:SEQ], w_conv[:, k, :], xt[:, 1 + k:1 + k + SEQ], start=k == 0, stop=k == TAPS - 1)
                        if k < TAPS - 1:
                            pe.quiet(step)
                        else:
                            conved = pe.do(step)
                    resed = pe.do(matmul(conv[:, SEQ:2 * SEQ], w_res[:], xt[:, 4:]))
                    yield
                    act.wait(resed)
                    if b >= NX:
                        yield from once(m, ("y_gated", b - NX))
                        act.wait(m["y_gated", b - NX])
                    act.tables(SILU)
                    xc_made = act.do(lambda e: e.activation(xc[i][:], conv[:, 0:SEQ], ACT.Silu, bias=conv_b))
                    m["sres", b] = act.do(lambda e: e.activation(sres[i][:], conv[:, SEQ:2 * SEQ], ACT.Silu))
                    banks.free(cn, m["sres", b])
                    yield
                    pe.wait(xc_made)
                    dt, dn = yield from banks.take(pe)
                    dted = pe.do(matmul(dt[:, 0:SEQ], w_dt[:], xc[i][:]))
                    yield
                    va, e_, u, lu, rl = sp_t
                    act.wait(dted)
                    if b:
                        act.wait(m["delta", b - 1])
                    absed = act.do(lambda e: e.activation(va[:], dt[:, 0:SEQ], ACT.Abs, bias=b_dt))
                    act.wait(absed)
                    act.tables(EXP_LN)
                    exped = act.do(lambda e: e.activation(e_[:], va[:], ACT.Exp, scale=-1.0))
                    dve.wait(absed)
                    relued = dve.do(lambda e: e.tensor_scalar(rl[:], dt[:, 0:SEQ], b_dt, 0.0, ALU.add, ALU.max))
                    yield
                    dve.wait(exped)
                    banks.free(dn, relued)
                    u_made = dve.do(lambda e: e.tensor_scalar(u[:], e_[:], 1.0, None, ALU.add))
                    act.wait(u_made)
                    act.tables(EXP_LN)
                    logged = act.do(lambda e: e.activation(lu[:], u[:], ACT.Ln))
                    dve.wait(u_made)
                    erred = dve.do(lambda e: e.scalar_tensor_tensor(out=va[:], in0=u[:], scalar=1.0, in1=e_[:],
                                                                    op0=ALU.subtract, op1=ALU.subtract))
                    dve.wait(erred, relued)
                    part = dve.do(lambda e: e.tensor_tensor(rl[:], rl[:], va[:], ALU.subtract))
                    yield
                    dve.wait(part, logged)
                    m["delta", b] = dve.do(lambda e: e.tensor_tensor(delta[i][:], rl[:], lu[:], ALU.add))
                    dve.wait(m["delta", b], xc_made)
                    m["dx", b] = dve.do(lambda e: e.tensor_tensor(dx[i][:], delta[i][:], xc[i][:], ALU.mult))
                    m["xc", b] = xc_made
                    yield

            scanned_by = [None] * ND
            summed_by = [None] * ND

            def scan():
                k = 0
                for b in range(SEQS):
                    i = b % NX
                    yield from once(m, ("dx", b))
                    y, yn = yield from banks.take(pe)
                    pe.wait(m["xc", b], mix_ready)
                    pe.quiet(matmul(y[:, 0:SEQ], mix_d[:, STATES, :], xc[i][:], start=True, stop=False))
                    scans = []
                    for s in range(STATES + 1):
                        if s < STATES:
                            j = k % ND
                            act.wait(m["delta", b], a_ready, *([scanned_by[j]] if scanned_by[j] else []))
                            act.tables(EXP_LN)
                            decayed = act.do(lambda e, s=s, j=j: e.activation(dA[j][:], delta[i][:], ACT.Exp, scale=neg_a[:, s:s + 1]))
                            dve.wait(decayed, m["dx", b], *([summed_by[j]] if summed_by[j] else []))
                            scanned = dve.do(lambda e, j=j: e.tensor_tensor_scan(hs[j][:], dA[j][:], dx[i][:], 0.0, ALU.mult, ALU.add))
                            scanned_by[j] = scanned
                            scans.append((j, scanned))
                            k += 1
                        if s >= 1:
                            j, scanned = scans[s - 1]
                            pe.wait(scanned)
                            summed = pe.do(matmul(y[:, 0:SEQ], mix_d[:, s - 1, :], hs[j][:], start=False, stop=s == STATES))
                            summed_by[j] = summed
                        if s % 2:
                            yield
                    dve.wait(summed, m["sres", b])
                    if b >= 2:
                        yield from once(m, ("z_used", b - 2))
                        dve.wait(m["z_used", b - 2])
                    gated = dve.do(lambda e: e.tensor_tensor(z[b % 2][:], y[:, 0:SEQ], sres[i][:], ALU.mult))
                    m["y_gated", b] = gated
                    banks.free(yn, gated)
                    yield

            def feed(lane):
                h = h0[lane]
                for b in range(lane, SEQS, 2):
                    i = b % NX
                    yield from once(m, ("y_gated", b))
                    pe.wait(m["y_gated", b])
                    o, n = yield from banks.take(pe)
                    projected = pe.do(matmul(o[:, 0:SEQ], w_out[:], z[lane][:]))
                    m["z_used", b] = projected
                    yield
                    dve.wait(projected)
                    added = dve.do(lambda e: e.tensor_tensor(r0[lane][:], o[:, 0:SEQ], x_in[i][:, 4:], ALU.add))
                    banks.free(n, added)
                    m["x_used", b] = added
                    x_a_ready = yield from layer_norm(r0[lane][:], added, lane, banks, x_a[lane][:])
                    yield
                    added = yield from ffn(w0, h, x_a[lane][:], x_a_ready, banks, (), r1[lane][:])
                    free = (m["mid", b - 2],) if b >= 2 else ()
                    normed = yield from layer_norm(r1[lane][:], added, lane, banks, x_b[lane][:], free)
                    sp.wait(normed)
                    m["mid", b] = out_slot[lane].start(sp, x_mid[:, b * SEQ:(b + 1) * SEQ], x_b[lane][:])
                    yield

            interleave([mixer_front(), scan(), feed(0), feed(1)])
            block0_stored = [m["mid", SEQS - 2], m["mid", SEQS - 1]]
            block0_ended = [(x.sem, x.count) for x in (pe, act, dve, pool)]

        for engine in (sp, pe, act, dve, pool):
            engine.wait(*block0_ended, *block0_stored)
        with ExitStack() as blk:
            sb1 = lambda name, shape: sb(name, shape, scope=blk)
            wq, _ = load("wq", [P, INNER], blk, 1)
            wk, _ = load("wk", [P, INNER], blk, 1)
            wv, _ = load("wv", [P, INNER], blk, 1)
            wg, _ = load("wg", [P, INNER], blk, 1)
            wo, _ = load("wo", [P, IC, P], blk, 1)
            esel, _ = load("esel", [P, IC, HEADS], blk, 1)
            mask, _ = load("mask", [P, QG], blk, 1)
            hv, _ = load("hv", [P, 2 * IC], blk, 1)
            mk, _ = load("mk", [HEADS * MEM, 2 * DH], blk, 1)
            w1 = load_ffn("f1", blk)
            w1_in = w1["in"]

            pre = sb1("pre", [P, P])
            post = sb1("post", [P, P])
            pre_zero = pool.do(lambda e: e.memset(pre[:], 0.0))
            post_zero = pool.do(lambda e: e.memset(post[:], 0.0))
            sp.wait(pre_zero, post_zero)
            mixes = Dma(sem("mixes_in"))
            for q in range(QG):
                s = slice(q * HEADS, (q + 1) * HEADS)
                mixes.start(sp, pre[s, s], d["preT"])
                mixes_in = mixes.start(sp, post[s, s], d["postT"])

            dve.wait(mixes_in)
            pre_ready = dve.do(lambda e: e.tensor_scalar(pre[:], pre[:], QK_SCALE, None, ALU.mult))

            LO = HALF * W_LO
            T8 = sb1("T8", [P, LO + HALF * W_HI + 4 * (W_HI + QG)])

            def row(g):
                return g * W_LO if g < HALF else LO + (g - HALF) * W_HI

            def scores(g, a=0, z=None):
                z = seen_by(g) if z is None else z
                return T8[:, row(g) + a:row(g) + z]

            SN = sb1("SN", [P, HEADS, KEYS])
            qz = sb1("qz", [P, HEADS, SEQ])
            kT = sb1("kT", [P, IC, KEYS])
            ktok = sb1("ktok", [P, 2, INNER])
            sq = [sb1(f"sq{i}", [P, 512]) for i in range(2)]
            qn = sb1("qn", [HEADS, SEQ])
            rq = sb1("rq", [P, 2 * HEADS])
            rk = sb1("rk", [P, 2 * HEADS])
            rk_sq = sb1("rk_sq", [P, 2 * HEADS])
            k_t = sb1("k_t", [P, 2 * HEADS])
            q_sq = sb1("q_sq", [P, 2 * HEADS])
            q_t = sb1("q_t", [P, 2 * HEADS])
            V = sb1("V", [P, 3, INNER])
            gate = sb1("gate", [P, IC, SEQ])
            AT0 = sb1("AT0", [P, HEADS, SEQ])
            N1 = SEQ - (HALF - 1) * QG
            AT1 = sb1("AT1", [P, HEADS, N1])
            AT2 = sb1("AT2", [MEM, HEADS, QG])
            NXB = 3
            xb = [sb1(f"xb{i}", [P, MEM + SEQ]) for i in range(NXB)]
            x_slot = [Dma(sem(f"xb{i}")) for i in range(NXB)]
            NE = 4
            E = [sb1(f"E{i}", [P, KEYS]) for i in range(NE)]
            W = [sb1(f"W{i}", [P, KEYS]) for i in range(2)]
            neg = [sb1(f"neg{i}", [P, P]) for i in range(2)]
            posts = [sb1(f"posts{i}", [P, P]) for i in range(NE)]
            top = [sb1(f"top{i}", [P, 8]) for i in range(4)]
            peak = sb1("peak", [P, GROUPS])
            total = sb1("total", [P, GROUPS])
            share = sb1("share", [P, GROUPS])
            r2 = sb1("r2", [P, SEQ])
            x_c = [sb1(f"x_c{i}", [P, SEQ]) for i in range(2)]
            r3 = sb1("r3", [P, SEQ])
            x_d = [sb1(f"x_d{i}", [P, SEQ]) for i in range(2)]
            y_slot = [Dma(sem(f"y_out{i}")) for i in range(2)]
            h1 = {"a": sb1("g_a", [P, HC, SEQ]), "b": sb1("g_b", [P, HC, SEQ]), "free": ()}
            group_slot = [Dma(sem(f"group_in{i}")) for i in range(8)]
            memv_slot = Dma(sem("memv_in"))

            zeroed = [pool.do(lambda e, t=t: e.memset(t, 0.0)) for t in
                      (T8[:], qz[:].rearrange("p h t -> p (h t)"), AT1[:].rearrange("p h t -> p (h t)"),
                       *(x[:, 0:MEM] for x in xb))]

            KM = HEADS * MEM
            dve.wait(w1_in)
            act.wait(w1_in)
            mks = act.do(lambda e: e.activation(sq[0][0:KM, 0:DH], mk[:, 0:DH], ACT.Square))
            dve.wait(mks)
            mkr = dve.do(lambda e: e.tensor_reduce(rk[0:KM, 0:1], sq[0][0:KM, 0:DH], mybir.AxisListType.X, ALU.add))
            dve.wait(mkr)
            mkr = dve.do(lambda e: e.tensor_scalar(rk[0:KM, 1:2], rk[0:KM, 0:1], NORM_EPS ** 2, None, ALU.max))
            for mkr in inverse_root(rk[0:KM, 1:2], mkr, rk[0:KM, 3:4], rk[0:KM, 2:3]):
                pass
            mkr = (pool.sem, pool.count)
            dve.wait(mkr)
            mkr = dve.do(lambda e: e.tensor_scalar(sq[1][0:KM, 0:P], mk[:], rk[0:KM, 3:4], None, ALU.mult))
            pe.wait(mkr)
            mkr = pe.do(lambda e: e.transpose(bank[0][:, 0:KM], sq[1][0:KM, 0:P], ident[0:KM, 0:KM]))
            dve.wait(mkr)
            for half in range(2):
                rows = slice(half * DH, (half + 1) * DH)
                src = bank[0][rows, 0:KM].rearrange("p (c two m) -> p c two m", two=2, m=MEM)[:, :, half, :]
                memk_ready = dve.do(lambda e, rows=rows, src=src: e.tensor_copy(kT[rows, :, 0:MEM], src))
            hh = sb1("hh", [P, 2 * IC])
            halved = dve.do(lambda e: e.tensor_scalar(hh[:], hv[:], 0.5, None, ALU.mult))
            dve.wait(halved)
            for c in range(IC):
                wo_ready = dve.do(lambda e, c=c: e.tensor_scalar(wo[:, c, :], wo[:, c, :], hh[:, c:c + 1], None, ALU.mult))

            banks, banksT = Banks(bank[0:6]), Banks(bank[6:8])
            banks.free(0, memk_ready)
            m = {}

            def attention_front():
                for b in range(SEQS):
                    x = xb[b % NXB]
                    if b >= NXB:
                        sp.wait((yield from once(m, ("x_used", b - NXB))))
                    loaded = x_slot[b % NXB].start(sp, x[:, MEM:], x_mid[:, b * SEQ:(b + 1) * SEQ])
                    pe.wait(loaded, w1_in, *zeroed)
                    q_sums, qsn = None, None
                    act.wait(zeroed[1])
                    for c2 in range(IC // 2):
                        o, n = yield from banks.take(pe)
                        for c in range(2):
                            at = (2 * c2 + c) * P
                            made = pe.do(matmul(o[:, c * SEQ:(c + 1) * SEQ], wq[:, at:at + P], x[:, MEM:]))
                        yield
                        s = sq[c2 % 2]
                        act.wait(made, *m.get(("sq_used", c2 % 2), ()))
                        squared = act.do(lambda e: e.activation(s[:], o[:], ACT.Square), 512)
                        if b and c2 == 0:
                            act.wait(m["s_made", b - 1])
                        for half in range(2):
                            rows = slice(half * DH, (half + 1) * DH)
                            dst = qz[rows, 4 * c2:4 * c2 + 4, :].rearrange("p (c two) t -> p c two t", two=2)[:, :, half, :]
                            src = o[rows, :].rearrange("p (c t) -> p c t", c=2)
                            copied = act.do(lambda e, dst=dst, src=src: e.activation(dst, src, ACT.Copy), 4 * P)
                        banks.free(n, copied)
                        pe.wait(squared)
                        if c2 == 0:
                            q_sums, qsn = yield from banks.take(pe)
                        for c in range(2):
                            cc = 2 * c2 + c
                            summed = pe.do(matmul(q_sums[0:HEADS, 0:SEQ], esel[:, cc, :], s[:, c * SEQ:(c + 1) * SEQ],
                                                  start=cc == 0, stop=cc == IC - 1))
                        m["sq_used", c2 % 2] = (summed,)
                        yield
                    act.wait(summed)
                    qn_made = act.do(lambda e: e.activation(qn[:], q_sums[0:HEADS, 0:SEQ], ACT.Copy))
                    banks.free(qsn, qn_made)
                    yield
                    pe.wait(qn_made)
                    o, n = yield from banks.take(pe)
                    for t in range(2):
                        turned = pe.do(lambda e, t=t: e.transpose(o[:, t * HEADS:(t + 1) * HEADS], qn[:, t * P:(t + 1) * P],
                                                                  ident[0:HEADS, 0:HEADS]))
                    yield
                    dve.wait(turned)
                    clipped = dve.do(lambda e: e.tensor_scalar(q_sq[:], o[:, 0:2 * HEADS], NORM_EPS ** 2, None, ALU.max), 32)
                    banks.free(n, clipped)
                    yield
                    if b:
                        act.wait(m["sn_made", b - 1])
                    rq_ready = yield from inverse_root(q_sq[:], clipped, rq[:], q_t[:])
                    for t in range(2):
                        norm, k_sq = (a[:, t * HEADS:(t + 1) * HEADS] for a in (rk, rk_sq))
                        halves = []
                        for f in range(2):
                            o, n = yield from banks.take(pe)
                            made = pe.do(matmul(o[:], x[:, MEM + t * P:MEM + (t + 1) * P], wk[:, f * 512:(f + 1) * 512]), 512)
                            s = sq[f]
                            act.wait(made, *m.get(("sq_used", f), ()))
                            squared = act.do(lambda e, s=s, o=o: e.activation(s[:], o[:], ACT.Square), 512)
                            yield
                            dve.wait(squared)
                            reduced = dve.do(lambda e, s=s, f=f: e.tensor_reduce(
                                k_sq[:, f * 8:(f + 1) * 8], s[:].rearrange("p (h d) -> p h d", d=DH), mybir.AxisListType.X, ALU.add), 512)
                            m["sq_used", f] = (reduced,)
                            halves.append((o, n, made))
                            yield
                        pool.wait(reduced)
                        clipped = pool.do(lambda e: e.tensor_scalar(k_sq, k_sq, NORM_EPS ** 2, 1.0, ALU.max, ALU.mult), 16)
                        rooted = yield from inverse_root(k_sq, clipped, norm, k_t[:, t * HEADS:(t + 1) * HEADS])
                        dve.wait(rooted)
                        if b:
                            dve.wait(m["k_turned", b - 1])
                        for f, (o, n, made) in enumerate(halves):
                            dst = ktok[:, t, f * 512:(f + 1) * 512].rearrange("p (h d) -> p h d", d=DH)
                            src = o[:].rearrange("p (h d) -> p h d", d=DH)
                            nrm = norm[:, f * 8:(f + 1) * 8].unsqueeze(2).to_broadcast([P, 8, DH])
                            scaled = dve.do(lambda e, dst=dst, src=src, nrm=nrm: e.tensor_tensor(dst, src, nrm, ALU.mult), 512)
                            banks.free(n, scaled)
                        yield
                        pe.wait(scaled)
                        for c4 in range(2):
                            o, n = yield from banks.take(pe)
                            for c in range(4):
                                at = (4 * c4 + c) * P
                                turned = pe.do(lambda e, o=o, c=c, at=at, t=t: e.transpose(
                                    o[:, c * P:(c + 1) * P], ktok[:, t, at:at + P], ident[:]), 60)
                            act.wait(turned)
                            if b:
                                act.wait(m["s_made", b - 1])
                            k_ready = act.do(lambda e, o=o, c4=c4, t=t: e.activation(
                                kT[:, 4 * c4:4 * c4 + 4, MEM + t * P:MEM + (t + 1) * P],
                                o[:].rearrange("p (c t) -> p c t", c=4), ACT.Copy), 512)
                            banks.free(n, k_ready)
                            yield
                    m["k_turned", b] = turned
                    for blk_q in range(2):
                        width = W_LO if blk_q == 0 else W_HI
                        per = 3 if blk_q == 0 else 1
                        pe.wait(k_ready, copied, memk_ready)
                        for h0_ in range(0, HEADS, per):
                            hs_ = range(h0_, min(h0_ + per, HEADS))
                            o, n = yield from banks.take(pe)
                            for j, h in enumerate(hs_):
                                made = pe.do(matmul(o[:, j * width:(j + 1) * width], qz[:, h, blk_q * P:(blk_q + 1) * P],
                                                    kT[:, h // 2, 0:width]), width)
                            act.wait(made, rq_ready)
                            if h0_ == 0 and ("sn_sent", b, blk_q) != ("sn_sent", 0, 0):
                                act.wait(*m["sn_sent"])
                            for j, h in enumerate(hs_):
                                c = blk_q * HEADS + h
                                evac = act.do(lambda e, o=o, j=j, h=h, c=c: e.activation(
                                    SN[:, h, 0:width], o[:, j * width:(j + 1) * width], ACT.Copy, scale=rq[:, c:c + 1]), width)
                            banks.free(n, evac)
                            yield
                        m["sn_made", b] = evac
                        if blk_q == 1:
                            m["s_made", b] = made
                        sp.wait(evac)
                        m["sn_sent"] = []
                        queued = []
                        for step in range(HALF + 2):
                            if step < HALF:
                                g = blk_q * HALF + step
                                if b:
                                    sp.wait((yield from once(m, ("mixed_back", b - 1, g))))
                                elif g == 0:
                                    sp.wait(zeroed[0])
                                slot = group_slot[g % 8]
                                sp.wait(*m.get(("slot_read", g % 8), ()))
                                sent = slot.start(sp, scores(g), SN[step * QG:(step + 1) * QG, :, 0:seen_by(g)])
                                m["sn_sent"].append(sent)
                                queued.append((g, sent))
                            if step >= 2:
                                g, sent = queued[step - 2]
                                pe.wait(sent, pre_ready)
                                o, n = yield from banks.take(pe)
                                mixed = pe.do(matmul(o[:, 0:seen_by(g)], pre[:], scores(g)), seen_by(g))
                                m["slot_read", g % 8] = (mixed,)
                                act.wait(mixed)
                                stored = act.do(lambda e, o=o, g=g: e.activation(scores(g), o[:, 0:seen_by(g)], ACT.Copy), seen_by(g))
                                banks.free(n, stored)
                                m["mixed", b, g] = stored
                            yield
                    yield

            def top_k():
                e_used = [None] * NE
                w_used = [None] * 2
                for b in range(SEQS):
                    def rank(g, k_top, b=b):
                        n_keys, s, first, j = seen_by(g), scores(g), top[k_top], g % NE
                        if b:
                            dve.wait(m["peak_read", b - 1])
                        dve.wait(m["scores", b, g])
                        best = dve.do(lambda e: e.max(first[:], s), n_keys)
                        yield
                        dve.wait(best)
                        peaked = dve.do(lambda e: e.tensor_scalar(peak[:, g:g + 1], first[:, 0:1], -1.0, None, ALU.mult), 1)
                        yield
                        if n_keys <= TOPK:
                            act.wait(peaked)
                            act.tables(EXP_LN)
                            summed = act.do(lambda e: e.activation(s, s, ACT.Exp, bias=peak[:, g:g + 1],
                                                                   accum_out=total[:, g:g + 1]), n_keys)
                            yield
                        else:
                            act.wait(peaked, *([e_used[j]] if e_used[j] else []))
                            act.tables(EXP_LN)
                            exped = act.do(lambda e: e.activation(E[j][:, 0:n_keys], s, ACT.Exp, bias=peak[:, g:g + 1]), n_keys)
                            below = n_keys - TOPK + 1
                            turn = below < TOPK
                            nth = below if turn else TOPK
                            base = s
                            if turn:
                                nt = neg[g % 2]
                                pool.wait(m["scores", b, g], *([w_used[g % 2]] if w_used[g % 2] else []))
                                turned = pool.do(lambda e: e.tensor_scalar(nt[:, 0:n_keys], s, -1.0, 1.0, ALU.mult, ALU.mult), n_keys)
                                base = nt[:, 0:n_keys]
                                dve.wait(turned, peaked)
                                best = dve.do(lambda e: e.max(first[:], base), n_keys)
                                yield
                            work = W[g % 2][:, 0:n_keys]
                            src = base
                            for _ in range((nth - 1) // 8):
                                dve.wait(best)
                                cut = dve.do(lambda e: e.match_replace(work, first[:], src, MASKED), n_keys)
                                yield
                                dve.wait(cut)
                                best = dve.do(lambda e: e.max(first[:], work), n_keys)
                                src = work
                                yield
                            at = (nth - 1) % 8
                            dve.wait(best, exped)
                            summed = dve.do(lambda e: e.scalar_tensor_tensor(
                                out=s, in0=base, scalar=first[:, at:at + 1], in1=E[j][:, 0:n_keys],
                                op0=ALU.is_le if turn else ALU.is_ge, op1=ALU.mult, accum_out=total[:, g:g + 1]), n_keys)
                            e_used[j] = summed
                            w_used[g % 2] = summed
                            yield
                        dve.wait(summed)
                        m["peak_read", b] = summed
                        m["share", b, g] = dve.do(lambda e: e.reciprocal(share[:, g:g + 1], total[:, g:g + 1]), 1)

                    masked = None
                    for g in range(0, GROUPS, 2):
                        for k in (g, g + 1):
                            yield from once(m, ("mixed", b, k))
                        if g % 4 == 0:
                            yield from once(m, ("mixed", b, g + 3))
                            stride = (W_LO if g < HALF else W_HI) + QG
                            at = row(g) + seen_by(g) - QG
                            tri = T8[:, at:at + 4 * stride].rearrange("p (g x) -> p g x", x=stride)[:, :, 0:QG]
                            dve.wait(m["mixed", b, g + 3])
                            masked = dve.do(lambda e: e.tensor_tensor(
                                tri, tri, mask[:].unsqueeze(1).to_broadcast([P, 4, QG]), ALU.add), 4 * QG)
                            for k in range(4):
                                m["scores", b, g + k] = masked
                        pair = [rank(g, 0), rank(g + 1, 1)]
                        while pair:
                            pair = [r for r in pair if next(r, "ended") != "ended"]
                            yield
                    yield

            def mix_turned():
                p_used = [None] * NE
                for b in range(SEQS):
                    def mix_back(g, ready, b=b):
                        j = g % NE
                        pool.wait(ready, mixes_in, *([p_used[j]] if p_used[j] else []))
                        scaled = pool.do(lambda e: e.tensor_scalar(posts[j][:], post[:], share[:, g:g + 1], 1.0, ALU.mult, ALU.mult), P)
                        pe.wait(scaled)
                        if g % 4 == 0:
                            m["at0"] = yield from banksT.take(pe)
                        o0, n0 = m["at0"]
                        turned = pe.do(matmul(o0[:, (g % 4) * P:(g % 4 + 1) * P], scores(g, 0, P), posts[j][:]), P)
                        if g >= HALF:
                            if g % 4 == 0:
                                m["at1"] = yield from banksT.take(pe)
                            o1, n1 = m["at1"]
                            turned = pe.do(matmul(o1[:, (g % 4) * P:(g % 4 + 1) * P], scores(g, P, 2 * P), posts[j][:]), P)
                        if g in (HALF - 1, GROUPS - 1):
                            o, n = yield from banks.take(pe)
                            a = P if g == HALF - 1 else 2 * P
                            turned = pe.do(matmul(o[0:MEM, 0:P], scores(g, a, a + MEM), posts[j][:]), P)
                            dst = AT1[0:MEM, :, 0:QG] if g == HALF - 1 else AT2[:]
                            src = o[0:MEM, 0:P].rearrange("p (q h) -> p h q", h=HEADS)
                            act.wait(turned)
                            if b:
                                act.wait(m["at_read", b - 1])
                            banks.free(n, act.do(lambda e: e.activation(dst, src, ACT.Copy), 4 * P))
                        m["mixed_back", b, g] = turned
                        p_used[j] = turned
                        return turned

                    def drain(g, turned, b=b):
                        if g % 4 != 3:
                            return
                        act.wait(turned)
                        if b:
                            act.wait(m["at_read", b - 1])
                        o0, n0 = m["at0"]
                        q0 = (g - 3) * QG
                        src = o0[:].rearrange("p (q h) -> p h q", h=HEADS)
                        done = act.do(lambda e: e.activation(AT0[:, :, q0:q0 + 4 * QG], src, ACT.Copy), 4 * P)
                        banksT.free(n0, done)
                        if g >= HALF:
                            o1, n1 = m["at1"]
                            q1 = q0 - (HALF - 1) * QG
                            src1 = o1[:].rearrange("p (q h) -> p h q", h=HEADS)
                            done = act.do(lambda e: e.activation(AT1[:, :, q1:q1 + 4 * QG], src1, ACT.Copy), 4 * P)
                            banksT.free(n1, done)
                        if g == GROUPS - 1:
                            m["at", b] = done

                    turned = {}
                    for g in range(GROUPS + 1):
                        if g % 4 == 0 and g:
                            if b:
                                yield from once(m, ("at_read", b - 1))
                            drain(g - 1, turned[g - 1])
                        if g < GROUPS:
                            yield from once(m, ("share", b, g))
                            turned[g] = yield from mix_back(g, m["share", b, g])
                        yield
                    yield

            def attention_back():
                for b in range(SEQS):
                    x = xb[b % NXB]
                    yield from once(m, ("s_made", b))
                    for t, size in ((0, P), (1, P), (2, MEM)):
                        for f in range(2):
                            o, n = yield from banks.take(pe)
                            made = pe.do(matmul(o[0:size, :], x[:, t * P:t * P + size], wv[:, f * 512:(f + 1) * 512]), 512)
                            yield
                            act.wait(made)
                            if b:
                                act.wait(m["at_read", b - 1])
                            v_made = act.do(lambda e, o=o, t=t, f=f, size=size: e.activation(
                                V[0:size, t, f * 512:(f + 1) * 512], o[0:size, :], ACT.Copy), 512)
                            banks.free(n, v_made)
                            yield
                        if t == 0:
                            sp.wait(v_made)
                            memv_ready = memv_slot.start(sp, V[0:MEM, 0, :], d["mem_v"])
                    for c2 in range(IC // 2):
                        o, n = yield from banks.take(pe)
                        for c in range(2):
                            at = (2 * c2 + c) * P
                            made = pe.do(matmul(o[:, c * SEQ:(c + 1) * SEQ], wg[:, at:at + P], x[:, MEM:]))
                        yield
                        act.wait(made, halved)
                        act.tables(SILU)
                        if b:
                            act.wait(m["ctx_read", b - 1])
                        for c in range(2):
                            cc = 2 * c2 + c
                            gate_ready = act.do(lambda e, o=o, c=c, cc=cc: e.activation(
                                gate[:, cc, :], o[:, c * SEQ:(c + 1) * SEQ], ACT.Tanh, bias=hh[:, IC + cc:IC + cc + 1], scale=0.5))
                        banks.free(n, gate_ready)
                        yield
                    at_ready = yield from once(m, ("at", b))
                    pe.wait(at_ready, v_made, memv_ready)
                    for c2 in range(IC // 2):
                        o, n = yield from banks.take(pe)
                        for c in range(2):
                            for half in range(2):
                                cc = 2 * c2 + c
                                h = 2 * cc + half
                                out_ = o[half * DH:(half + 1) * DH, c * SEQ:(c + 1) * SEQ]
                                cols = slice(h * DH, (h + 1) * DH)
                                pe.quiet(matmul(out_, V[:, 0, cols], AT0[:, h, :], start=True, stop=False))
                                pe.quiet(matmul(out_[:, SEQ - N1:SEQ], V[:, 1, cols], AT1[:, h, :], start=False, stop=False))
                                made = pe.do(matmul(out_[:, SEQ - QG:SEQ], V[0:MEM, 2, cols], AT2[:, h, :], start=False, stop=True))
                        if c2 == IC // 2 - 1:
                            m["at_read", b] = made
                        yield
                        dve.wait(made, gate_ready)
                        view = gate[:, 2 * c2:2 * c2 + 2, :].rearrange("p c t -> p (c t)")
                        gated = dve.do(lambda e, o=o, view=view: e.scalar_tensor_tensor(
                            out=view, in0=view, scalar=1.0, in1=o[:], op0=ALU.add, op1=ALU.mult), 512)
                        banks.free(n, gated)
                        yield
                    pe.wait(gated, wo_ready)
                    o, n = yield from banks.take(pe)
                    for c in range(IC):
                        step = matmul(o[:, 0:SEQ], wo[:, c, :], gate[:, c, :], start=c == 0, stop=c == IC - 1)
                        if c < IC - 1:
                            pe.quiet(step)
                        else:
                            made = pe.do(step)
                    m["ctx_read", b] = made
                    yield
                    dve.wait(made)
                    added = dve.do(lambda e, o=o: e.tensor_tensor(r2[:], o[:, 0:SEQ], x[:, MEM:], ALU.add))
                    banks.free(n, added)
                    m["x_used", b] = added
                    free = ()
                    if b >= 2:
                        yield from once(m, ("x_c_used", b - 2))
                        free = (m["x_c_used", b - 2],)
                    m["x_c", b] = yield from layer_norm(r2[:], added, 0, banks, x_c[b % 2][:], free)
                    yield

            def feed():
                for b in range(SEQS):
                    yield from once(m, ("x_c", b))
                    added = yield from ffn(w1, h1, x_c[b % 2][:], m["x_c", b], banks, (), r3[:])
                    m["x_c_used", b] = added
                    free = (m["y", b - 2],) if b >= 2 else ()
                    normed = yield from layer_norm(r3[:], added, 1, banks, x_d[b % 2][:], free)
                    sp.wait(normed)
                    m["y", b] = y_slot[b % 2].start(sp, out[:, b * SEQ:(b + 1) * SEQ], x_d[b % 2][:])
                    yield

            interleave([top_k(), attention_front(), mix_turned(), attention_back(), feed()])
            sp.wait(m["y", SEQS - 2], m["y", SEQS - 1])


def lay_out(i):
    a = {}
    as_is = lambda x: np.ascontiguousarray(np.asarray(x))
    a["xT"] = as_is(np.asarray(i["L0_attn_x"]).reshape(SEQS * SEQ, P).T)
    w_in = np.asarray(i["L0_attn_W_in"])
    a["w_in"], a["w_resT"] = as_is(w_in[:P]), as_is(w_in[P:].T)
    a["w_dtT"], a["w_outT"] = as_is(np.asarray(i["L0_attn_W_dt"]).T), as_is(np.asarray(i["L0_attn_W_out"]).T)
    col = lambda n: np.asarray(i[n]).reshape(-1, 1)
    a["vec"] = np.concatenate([np.asarray(i["L0_attn_conv_w"]), col("L0_attn_conv_b"), col("L0_attn_b_dt"), col("L0_attn_Dp")], 1)
    a["ssm"] = np.concatenate([np.asarray(i[f"L0_attn_{n}"]) for n in ("A_log", "Bp", "Cp")], 1)
    by_chunk = lambda x: np.asarray(x).reshape(-1, P).T
    for b in (0, 1):
        f = lambda n: np.asarray(i[f"L{b}_ffn_{n}"])
        a[f"f{b}w1"], a[f"f{b}w2"] = as_is(f("w1_w").T), as_is(f("w2_w").T)
        for n in ("h1", "h2"):
            a[f"f{b}{n}"] = as_is(f(n + "_w").T.reshape(HC, P, HID).transpose(1, 0, 2))
        a[f"f{b}w3"] = as_is(f("w3_w").T.reshape(HC, P, P).transpose(1, 0, 2))
        a[f"f{b}s"] = np.concatenate([by_chunk(f(n + "_s")) for n in ("w1", "w2", "h1", "h2", "w3")], 1)
    g = lambda n: np.asarray(i[f"L1_attn_{n}"])
    for n in ("q", "k", "v", "g"):
        a["w" + n] = as_is(g("W" + n))
    a["wo"] = as_is(g("Wo").reshape(IC, P, P).transpose(1, 0, 2))
    a["preT"], a["postT"] = as_is(g("W_pre_th").T), as_is(g("W_post_th").T)
    mk = g("mem_k").reshape(HEADS * MEM, DH)
    a["mk"] = np.concatenate([mk, mk], 1)
    a["mem_v"] = as_is(g("mem_v").transpose(1, 0, 2).reshape(MEM, INNER))
    scale = np.broadcast_to(g("head_scale_params").reshape(HEADS, 1), (HEADS, DH))
    a["hv"] = np.concatenate([by_chunk(as_is(scale)), by_chunk(g("bg"))], 1)
    a["ident"] = np.eye(P, dtype=np.float32)
    a["meanmat"] = np.full((P, P), 1.0 / P, np.float32)
    esel = np.zeros((P, IC, HEADS), np.float32)
    for c in range(IC):
        esel[:DH, c, 2 * c] = 1.0
        esel[DH:, c, 2 * c + 1] = 1.0
    a["esel"] = esel
    query = np.arange(P)[:, None] // HEADS
    a["mask"] = np.where(np.arange(QG)[None, :] > query, np.float32(MASKED), np.float32(0.0)).astype(np.float32)
    return {n: np.ascontiguousarray(x) for n, x in a.items()}


def kernel(**inputs):
    import concourse.bacc as bacc
    from concourse.bass_utils import run_bass_kernel_spmd

    nc = bacc.Bacc("TRN2", target_bir_lowering=False, num_devices=1)
    arrays = lay_out(inputs)
    d = {n: nc.dram_tensor("in_" + n, a.shape, mybir.dt.from_np(a.dtype), kind="ExternalInput").ap()
         for n, a in arrays.items()}
    out = nc.dram_tensor("out_y", [P, SEQS * SEQ], F32, kind="ExternalOutput").ap()
    program(nc, d, out)
    r = run_bass_kernel_spmd(nc, [{"in_" + n: a for n, a in arrays.items()}], core_ids=[0])
    y = np.asarray(r.results[0]["out_y"])
    return np.ascontiguousarray(y.T).reshape(SEQS, SEQ, P)
```
